# Optimizing a Trainium2 kernel written in Bass

```python
import numpy as np
import jax
import jax.numpy as jnp

def _softmax(x, axis=-1):
    return jax.nn.softmax(x, axis=axis)

def _gelu(x):
    return jax.nn.gelu(x, approximate=True)

def _silu(x):
    return jax.nn.silu(x)

def _sigmoid(x):
    return jax.nn.sigmoid(x)

def _layernorm(x, axis=-1, eps=1e-05):
    m = jnp.mean(x, axis=axis, keepdims=True)
    v = jnp.var(x, axis=axis, keepdims=True)
    return (x - m) / jnp.sqrt(v + eps)

def _scatter_add(tgt, idx, src, axis=0):
    return tgt.at[idx].add(src)

def _segment_sum(src, seg, n):
    return jax.ops.segment_sum(src, seg, n)
kernel_name = 'mk_vit_tower_d1_tok_img768_r4_859951'

def setup_inputs(seed: int=0):
    np.random.seed(seed)
    _w = jnp.asarray

    def _rec_inputs():
        import jax
        import jax.numpy as jnp
        _rk = jax.random.key(seed)
        x = -0.000222058 + 0.999998 * jax.random.normal(jax.random.fold_in(_rk, 1), (16, 3, 112, 112), jnp.float32)
        return x
    x = _rec_inputs()

    def _L0_tok_setup():
        import jax, jax.numpy as jnp
        import numpy as np
        from jax import lax
        HIDDEN = 192
        C_IN = 3
        PATCH = 16
        SIDE = 32
        NUM_PATCHES = SIDE * SIDE

        def _position_ids(nb_h, nb_w):
            boundaries = np.arange(1.0 / SIDE, 1.0, 1.0 / SIDE, dtype=np.float32)
            frac_h = np.arange(0.0, 1.0 - 1e-06, 1.0 / nb_h, dtype=np.float32)
            frac_w = np.arange(0.0, 1.0 - 1e-06, 1.0 / nb_w, dtype=np.float32)
            bh = np.searchsorted(boundaries, frac_h, side='right')
            bw = np.searchsorted(boundaries, frac_w, side='right')
            return jnp.asarray((bh[:, None] * SIDE + bw).reshape(-1), dtype=jnp.int32)
        key = jax.random.key(seed)
        k1, k2, k3 = jax.random.split(key, 3)
        pixel_values = jax.random.normal(k1, (32, C_IN, 128, 128), dtype=jnp.float32)
        conv_w = jax.random.normal(k2, (HIDDEN, C_IN, PATCH, PATCH), dtype=jnp.float32) * 0.02
        conv_b = jnp.zeros((HIDDEN,), dtype=jnp.float32)
        pos_table = jax.random.normal(k3, (NUM_PATCHES, HIDDEN), dtype=jnp.float32) * 0.02
        return {'pixel_values': pixel_values, 'conv_w': conv_w, 'conv_b': conv_b, 'pos_table': pos_table}
    _L0_tok_all = _L0_tok_setup()
    _L0_tok_in = {k: v for k, v in _L0_tok_all.items() if k in ('conv_w', 'conv_b', 'pos_table')}
    del _L0_tok_all

    def _L0_attn_setup():
        import jax, jax.numpy as jnp
        import numpy as np
        D_HEAD = 64
        IGNORE = -100000.0
        key = jax.random.key(seed)
        ks = jax.random.split(key, 5)
        B, S, D, H, M = (2, 512, 192, 12, D_HEAD)
        scale = 0.05
        return {'x': jax.random.normal(ks[0], (B, S, D), jnp.float32), 'W_Q': jax.random.normal(ks[1], (H, D, M), jnp.float32) * scale, 'b_Q': jnp.zeros((H, M), jnp.float32), 'W_K': jax.random.normal(ks[2], (H, D, M), jnp.float32) * scale, 'b_K': jnp.zeros((H, M), jnp.float32), 'W_V': jax.random.normal(ks[3], (H, D, M), jnp.float32) * scale, 'b_V': jnp.zeros((H, M), jnp.float32), 'W_O': jax.random.normal(ks[4], (H, M, D), jnp.float32) * scale, 'b_O': jnp.zeros((D,), jnp.float32)}
    _L0_attn_all = _L0_attn_setup()
    _L0_attn_in = {k: v for k, v in _L0_attn_all.items() if k in ('W_Q', 'b_Q', 'W_K', 'b_K', 'W_V', 'b_V', 'W_O', 'b_O')}
    del _L0_attn_all

    def _L0_ffn_setup():
        import jax, jax.numpy as jnp
        import numpy as np
        import math
        B, S, D = (4, 1024, 192)
        E = 8
        TOP_K = 2
        H = 512
        CAP_F = 1.25
        EPS = 1e-06
        ALPHA = 1.0
        key = jax.random.key(seed)
        k0, k1, k2, k3 = jax.random.split(key, 4)
        x = jax.random.normal(k0, (B, S, D), jnp.float32)
        gate_w = jax.random.normal(k1, (E, D), jnp.float32) * 0.02
        w13 = jax.random.normal(k2, (E, 2 * H, D), jnp.float32) * 0.02
        w2 = jax.random.normal(k3, (E, D, H), jnp.float32) * 0.02
        norm_w = jnp.ones((E, D), jnp.float32)
        return {'x': x, 'gate_w': gate_w, 'w13': w13, 'w2': w2, 'norm_w': norm_w}
    _L0_ffn_all = _L0_ffn_setup()
    _L0_ffn_in = {k: v for k, v in _L0_ffn_all.items() if k in ('gate_w', 'w13', 'w2', 'norm_w')}
    del _L0_ffn_all
    return {'x': x, 'L0_tok_conv_w': _L0_tok_in['conv_w'], 'L0_tok_conv_b': _L0_tok_in['conv_b'], 'L0_tok_pos_table': _L0_tok_in['pos_table'], 'L0_attn_W_Q': _L0_attn_in['W_Q'], 'L0_attn_b_Q': _L0_attn_in['b_Q'], 'L0_attn_W_K': _L0_attn_in['W_K'], 'L0_attn_b_K': _L0_attn_in['b_K'], 'L0_attn_W_V': _L0_attn_in['W_V'], 'L0_attn_b_V': _L0_attn_in['b_V'], 'L0_attn_W_O': _L0_attn_in['W_O'], 'L0_attn_b_O': _L0_attn_in['b_O'], 'L0_ffn_gate_w': _L0_ffn_in['gate_w'], 'L0_ffn_w13': _L0_ffn_in['w13'], 'L0_ffn_w2': _L0_ffn_in['w2'], 'L0_ffn_norm_w': _L0_ffn_in['norm_w']}

def reference(x, L0_tok_conv_w, L0_tok_conv_b, L0_tok_pos_table, L0_attn_W_Q, L0_attn_b_Q, L0_attn_W_K, L0_attn_b_K, L0_attn_W_V, L0_attn_b_V, L0_attn_W_O, L0_attn_b_O, L0_ffn_gate_w, L0_ffn_w13, L0_ffn_w2, L0_ffn_norm_w):
    import jax
    import jax.numpy as jnp

    def _L0_tok_ref(pixel_values, conv_w, conv_b, pos_table):
        import jax, jax.numpy as jnp
        import numpy as np
        from jax import lax
        HIDDEN = 192
        C_IN = 3
        PATCH = 16
        SIDE = 32
        NUM_PATCHES = SIDE * SIDE

        def _position_ids(nb_h, nb_w):
            boundaries = np.arange(1.0 / SIDE, 1.0, 1.0 / SIDE, dtype=np.float32)
            frac_h = np.arange(0.0, 1.0 - 1e-06, 1.0 / nb_h, dtype=np.float32)
            frac_w = np.arange(0.0, 1.0 - 1e-06, 1.0 / nb_w, dtype=np.float32)
            bh = np.searchsorted(boundaries, frac_h, side='right')
            bw = np.searchsorted(boundaries, frac_w, side='right')
            return jnp.asarray((bh[:, None] * SIDE + bw).reshape(-1), dtype=jnp.int32)
        B, _, H, W = pixel_values.shape
        nb_h, nb_w = (H // PATCH, W // PATCH)
        patches = lax.conv_general_dilated(pixel_values, conv_w, window_strides=(PATCH, PATCH), padding='VALID', dimension_numbers=('NCHW', 'OIHW', 'NCHW'))
        patches = patches + conv_b[None, :, None, None]
        embeddings = patches.reshape(B, HIDDEN, nb_h * nb_w).transpose(0, 2, 1)
        pos_ids = _position_ids(nb_h, nb_w)
        pos_emb = pos_table[pos_ids]
        return embeddings + pos_emb[None, :, :]

    def _L0_attn_ref(x, W_Q, b_Q, W_K, b_K, W_V, b_V, W_O, b_O):
        import jax, jax.numpy as jnp
        import numpy as np
        D_HEAD = 64
        IGNORE = -100000.0
        q = jnp.einsum('bqd,hdm->bqhm', x, W_Q) + b_Q
        k = jnp.einsum('bkd,hdm->bkhm', x, W_K) + b_K
        v = jnp.einsum('bkd,hdm->bkhm', x, W_V) + b_V
        scores = jnp.einsum('bqhm,bkhm->bhqk', q, k) / jnp.sqrt(jnp.asarray(D_HEAD, q.dtype))
        S = x.shape[1]
        causal = jnp.arange(S)[:, None] >= jnp.arange(S)[None, :]
        scores = jnp.where(causal[None, None, :, :], scores, jnp.asarray(IGNORE, scores.dtype))
        pattern = jax.nn.softmax(scores, axis=-1)
        z = jnp.einsum('bhqk,bkhm->bqhm', pattern, v)
        attn_out = jnp.einsum('bqhm,hmd->bqd', z, W_O) + b_O
        return attn_out

    def _L0_ffn_ref(x, gate_w, w13, w2, norm_w):
        import jax, jax.numpy as jnp
        import numpy as np
        import math
        B, S, D = (4, 1024, 192)
        E = 8
        TOP_K = 2
        H = 512
        CAP_F = 1.25
        EPS = 1e-06
        ALPHA = 1.0
        Bx, Sx, Dx = x.shape
        N = Bx * Sx
        cap = int(math.ceil(CAP_F * TOP_K * N / E))
        xf = x.reshape(N, Dx)
        logits = xf.astype(jnp.float32) @ gate_w.T
        probs = jax.nn.softmax(logits, axis=-1)
        top_p, top_i = jax.lax.top_k(probs, TOP_K)
        w = top_p / jnp.sum(top_p, axis=-1, keepdims=True)
        flat_e = top_i.reshape(-1)
        onehot = jax.nn.one_hot(flat_e, E, dtype=jnp.int32)
        pos = jnp.take_along_axis(jnp.cumsum(onehot, axis=0) - 1, flat_e[:, None], axis=1)[:, 0]
        keep = pos < cap
        didx = flat_e * cap + jnp.minimum(pos, cap - 1)
        safe = jnp.where(keep, didx, E * cap)
        x_rep = jnp.repeat(xf, TOP_K, axis=0)
        buf = jnp.zeros((E * cap + 1, Dx), x.dtype).at[safe].set(x_rep)
        buf = buf[:-1].reshape(E, cap, Dx)
        z = 2.0 * buf
        z = z * jax.lax.rsqrt(jnp.mean(z * z, axis=-1, keepdims=True) + EPS)
        z = z * norm_w[:, None, :]
        gu = jnp.einsum('ecd,ehd->ech', z, w13)
        g, u = jnp.split(gu, 2, axis=-1)
        y = buf + ALPHA * jnp.einsum('ech,edh->ecd', jax.nn.silu(g) * u, w2)
        y_tok = y.reshape(E * cap, Dx)[didx]
        cw = (w.reshape(-1) * keep.astype(w.dtype)).astype(x.dtype)
        out = (cw[:, None] * y_tok).reshape(N, TOP_K, Dx).sum(axis=1)
        return out.reshape(Bx, Sx, Dx)
    h = _L0_tok_ref(x, L0_tok_conv_w, L0_tok_conv_b, L0_tok_pos_table)
    h = h + _L0_attn_ref(_layernorm(h, axis=-1), L0_attn_W_Q, L0_attn_b_Q, L0_attn_W_K, L0_attn_b_K, L0_attn_W_V, L0_attn_b_V, L0_attn_W_O, L0_attn_b_O)
    h = h + _L0_ffn_ref(_layernorm(h, axis=-1), L0_ffn_gate_w, L0_ffn_w13, L0_ffn_w2, L0_ffn_norm_w)
    return h

_drawn_inputs = setup_inputs


def setup_inputs(seed=0):
    import zlib

    import numpy as np

    out = dict(_drawn_inputs(seed))
    spreads = {'L0_tok_conv_b': (0.0, 0.1),
     'L0_attn_b_Q': (0.0, 0.1),
     'L0_attn_b_K': (0.0, 0.8),
     'L0_attn_b_V': (0.0, 0.1),
     'L0_attn_b_O': (0.0, 0.1),
     'L0_ffn_norm_w': (1.0, 0.6)}
    factors = {'L0_ffn_w13': 6.888, 'L0_ffn_w2': 6.884}
    for name, (base, spread) in spreads.items():
        noise = np.random.default_rng([zlib.crc32(name.encode()), seed]).standard_normal(out[name].shape)
        drawn = base * np.exp(spread * noise) if base else spread * noise
        out[name] = jnp.asarray(drawn.astype(out[name].dtype))
    for name, factor in factors.items():
        out[name] = (out[name] * factor).astype(out[name].dtype)
    return out
```

```python
from contextlib import ExitStack

import numpy as np
import concourse.bass as bass
from concourse import mybir

IMAGES, CHANNELS, SIDE, PATCH = 16, 3, 112, 16
PER_SIDE = SIDE // PATCH
TOK = PER_SIDE * PER_SIDE
D = 192
HEADS, DH = 12, 64
HP = HEADS // 2
EXPERTS, TOPK, HID = 8, 2, 512
N = IMAGES * TOK
CAP = -(-5 * TOPK * N // (4 * EXPERTS))
GRID = 32

PT = 2 * TOK
PAIRS = IMAGES // 2
PH = 4
HALVES = PAIRS // PH
SLOT = 64
CK = D // 2
KC = CHANNELS * PATCH * PATCH // 128
STRIDE = 256
EROWS = (CAP + 1) // 2
EC = 2 * EROWS
JT = HID // 128
FAR = float(1 << 20)
LN_EPS, RMS_EPS = 1e-5, 1e-6
IGNORE = -100000.0


def vit_block(nc, patches, conv_w, conv_b, pos, w_q, w_k, w_v, w_o, b_q, b_k, b_v, b_o, gate, w13, w2,
              eye, causal, before, expert_no, out):
    f32, bf16, u32 = mybir.dt.float32, mybir.dt.bfloat16, mybir.dt.uint32
    ALU, ACT, AX = mybir.AluOpType, mybir.ActivationFunctionType, mybir.AxisListType

    slot_x = nc.dram_tensor("slot_x", [EXPERTS * STRIDE, D], f32, kind="Internal").ap()
    slot_y = nc.dram_tensor("slot_y", [EXPERTS * STRIDE, D], f32, kind="Internal").ap()

    with ExitStack() as ctx:
        def sb(name, shape, dt=f32):
            return ctx.enter_context(nc.sbuf_tensor(name, shape, dt))

        def sem(name):
            return ctx.enter_context(nc.semaphore(name))

        convw = sb("convw", [128, KC, D])
        posb = sb("posb", [PT, D])
        convb = sb("convb", [PT, D])
        wq = sb("wq", [CK, 2, HEADS * DH])
        wk = sb("wk", [CK, 2, HEADS * DH])
        wv = sb("wv", [CK, 2, HEADS * DH])
        wo = sb("wo", [128, HP, D])
        bq = sb("bq", [128, HP])
        bk = sb("bk", [128, HP])
        bv = sb("bv", [128, HP])
        bo = sb("bo", [PT, D])
        gatew = sb("gatew", [CK, 2, EXPERTS])
        ident = sb("ident", [128, 128])
        mask = sb("mask", [128, TOK])
        earlier = sb("earlier", [PT, PT], bf16)
        ones = sb("ones", [PT, PT], bf16)
        eno = sb("eno", [PT, TOPK, EXPERTS])
        mhalf = sb("mhalf", [PT, 1])
        zeros = sb("zeros", [128, EXPERTS * STRIDE * D // 512])
        xp = sb("xp", [128, PH, KC, PT])
        h = sb("h", [PT, PH, D])
        hb = sb("hb", [PT, PH, D])
        y = sb("y", [PT, 2, D])
        yT = sb("yT", [CK, 2, PH, 128])
        qT = sb("qT", [128, HP, PH, 2, SLOT])
        kB = sb("kB", [128, HP, PH, 2, 2, TOK])
        v = sb("v", [128, PH, HEADS * DH])
        stats = sb("stats", [PT, 2, 6])
        mv = sb("mv", [PT, 2, 2])
        ve = sb("ve", [PT, 2])
        rstd = sb("rstd", [PT, 2])
        sm = sb("sm", [128, 2, HEADS, TOK])
        sx = sb("sx", [128, 2, HEADS, TOK])
        prob = sb("prob", [128, 2, HEADS, SLOT])
        smax = sb("smax", [128, 2, HEADS])
        ssum = sb("ssum", [128, 2, HEADS])
        srec = sb("srec", [128, 2, HEADS])
        probT = sb("probT", [128, HEADS, 2, TOK])
        zT = sb("zT", [128, 2, HP, PT])
        h2 = sb("h2", [PT, PH, D])
        y2 = sb("y2", [PT, PH, D])
        y2T = sb("y2T", [CK, 2, PT])
        sq = sb("sq", [PT, D])
        ssq = sb("ssq", [PT, 2])
        msq = sb("msq", [PT, 2])
        rrms = sb("rrms", [PT, 2])
        stats2 = sb("stats2", [PT, 2, 6])
        mv2 = sb("mv2", [PT, 2, 2])
        ve2 = sb("ve2", [PT, 2])
        rstd2 = sb("rstd2", [PT, 2])
        zn = sb("zn", [PT, PH, D])
        lg = sb("lg", [PT, 2, EXPERTS])
        top = sb("top", [PT, 2, 8])
        topi = sb("topi", [PT, 2, 8], u32)
        chosen = sb("chosen", [PT, 2, TOPK])
        oneh = sb("oneh", [PT, 2, TOPK, EXPERTS])
        both = sb("both", [PT, 2, EXPERTS], bf16)
        seen = sb("seen", [PT, EXPERTS], bf16)
        gap = sb("gap", [PT, 2])
        ratio = sb("ratio", [PT, 2])
        picked = sb("picked", [PT, TOPK, EXPERTS])
        place = sb("place", [PT, TOPK])
        kept = sb("kept", [PT, TOPK])
        far = sb("far", [PT, TOPK])
        slotf = sb("slotf", [PT, TOPK])
        slotg = sb("slotg", [PT, TOPK])
        slot = sb("slot", [PT, PH, TOPK], u32)
        wsum = sb("wsum", [PT, 1])
        share = sb("share", [PT, TOPK])
        cw = sb("cw", [PT, TOPK])
        csum = sb("csum", [PT, 1])
        slot_all = sb("slot_all", [PT, PAIRS, TOPK], u32)
        cw_all = sb("cw_all", [PT, PAIRS, TOPK])
        base = sb("base", [PT, PAIRS, D])
        W13 = 2 * HID
        w13s = sb("w13s", [CK, 2, 2 * W13 + 2])
        w2s = sb("w2s", [128, 2, JT, D])
        xe = sb("xe", [128, 2, 2, D])
        zeT = sb("zeT", [CK, 2, 2, EC])
        sg = sb("sg", [128, 4, EC])
        hT = sb("hT", [128, 2, JT, EC])
        ye = sb("ye", [128, 2, 2, D])
        got = sb("got", [PT, PAIRS, TOPK, D])
        part = sb("part", [PT, 2, D])
        res = sb("res", [PT, PAIRS, D])

        ps = ctx.enter_context(nc.psum_tensor("ps", [128, 8, 512], f32))

        ld_conv, ld_qkv, ld_wo, ld_const, ld_gate = (sem(f"ld_{x}") for x in ("conv", "qkv", "wo", "const", "gate"))
        ld_x = [sem(f"ld_x{p}") for p in range(PH)]
        ld_w = [sem(f"ld_w{j}") for j in range(2)]
        ld_e = [sem(f"ld_e{j}") for j in range(2)]
        zeroed = sem("zeroed")
        posb_ready, sets, cleared = sem("posb_ready"), sem("sets"), sem("cleared")
        conv_done, yt_done, v_done, qk_done = (sem(x) for x in ("conv_done", "yt_done", "v_done", "qk_done"))
        s_done, pt_done, z_done, wo_done = (sem(x) for x in ("s_done", "pt_done", "z_done", "wo_done"))
        y2t_done, lg_done, before_done = (sem(x) for x in ("y2t_done", "lg_done", "before_done"))
        h_ready, mv_ready, rstd_ready, y_ready, hb_ready = (sem(x) for x in ("h_ready", "mv_ready", "rstd_ready", "y_ready", "hb_ready"))
        yT_ready, v_ready, q_ready, k_ready = (sem(x) for x in ("yT_ready", "v_ready", "q_ready", "k_ready"))
        sm_ready, sx_ready, exp_ready, p_ready = (sem(x) for x in ("sm_ready", "sx_ready", "exp_ready", "p_ready"))
        pta_ready, ptd_ready, z_ready = (sem(x) for x in ("pta_ready", "ptd_ready", "z_ready"))
        h2_ready, mv2_ready, rstd2_ready, y2_ready = (sem(x) for x in ("h2_ready", "mv2_ready", "rstd2_ready", "y2_ready"))
        y2T_ready, ssq_ready, rrms_ready, zn_ready = (sem(x) for x in ("y2T_ready", "ssq_ready", "rrms_ready", "zn_ready"))
        lg_ready, both_ready, gap_ready, ratio_ready = (sem(x) for x in ("lg_ready", "both_ready", "gap_ready", "ratio_ready"))
        before_read, slot_ready, seen_ready, base_ready = (sem(x) for x in ("before_read", "slot_ready", "seen_ready", "base_ready"))
        scattered = [[sem(f"scattered{p}{k}") for k in range(TOPK)] for p in range(PH)]
        sent = sem("sent")
        dve_seq, pool_seq = sem("dve_seq"), sem("pool_seq")
        held = sem("held")
        et_done, gu_done, down_done = sem("et_done"), sem("gu_done"), sem("down_done")
        zeT_ready, sg_ready, hT_ready, ye_ready = (sem(x) for x in ("zeT_ready", "sg_ready", "hT_ready", "ye_ready"))
        stored = [sem(f"stored{j}") for j in range(2)]
        gathered = [sem(f"gathered{t}") for t in range(PAIRS)]
        part_ready, res_ready, out_done = sem("part_ready"), sem("res_ready"), sem("out_done")

        compute = (sent, base_ready, before_done, before_read, both_ready, conv_done, down_done, et_done, exp_ready, gap_ready, gu_done, h2_ready, hT_ready, h_ready, hb_ready, k_ready, lg_done, lg_ready, mv2_ready, mv_ready, p_ready, pt_done, pta_ready, ptd_ready, q_ready, qk_done, ratio_ready, rrms_ready, rstd2_ready, rstd_ready, s_done, seen_ready, sg_ready, slot_ready, sm_ready, ssq_ready, sx_ready, v_done, v_ready, wo_done, y2T_ready, y2_ready, y2t_done, yT_ready, y_ready, ye_ready, yt_done, z_done, z_ready, zeT_ready, zn_ready)
        CONST_LOADS = 11
        block = ctx.enter_context(nc.Block())

        @block.sync
        def _(sp):
            def load_x(p, pair):
                sp.dma_start(xp[:, p], patches[pair]).then_inc(ld_x[p], 16)

            def load_expert(j, e):
                sp.dma_start(w13s[:, j], w13[e]).then_inc(ld_w[j], 16)
                sp.dma_start(w2s[:, j], w2[e]).then_inc(ld_w[j], 16)

            def load_slots(j, e):
                sp.dma_start(xe[:, j], slot_x[bass.ds(e * STRIDE, STRIDE), :].rearrange("(p two) d -> p two d", two=2)).then_inc(ld_e[j], 16)

            def store_expert(j, e):
                sp.dma_start(slot_y[bass.ds(e * STRIDE, STRIDE), :].rearrange("(p two) d -> p two d", two=2), ye[:, j]).then_inc(stored[j], 16)

            sp.dma_start(convw[:], conv_w).then_inc(ld_conv, 16)
            for c in compute:
                sp.sem_inc(c, 1)
            for c in stored:
                sp.sem_inc(c, 16)
            load_x(0, 0)
            load_x(1, 1)
            load_x(2, 2)
            load_x(3, 3)
            sp.dma_start(wv[:], w_v).then_inc(ld_qkv, 16)
            sp.dma_start(wq[:], w_q).then_inc(ld_qkv, 16)
            sp.dma_start(wk[:], w_k).then_inc(ld_qkv, 16)
            sp.dma_start(wo[:], w_o).then_inc(ld_wo, 16)
            load_expert(0, 0)
            load_expert(1, 1)
            sp.wait_ge(cleared, 1)
            for q in range(4):
                sp.dma_start(slot_x.rearrange("(q p r) d -> q p (r d)", q=4, p=128)[q], zeros[:]).then_inc(zeroed, 16)
            for p in range(PH):
                sp.wait_ge(conv_done, 1 + p + 1)
                load_x(p, PH + p)
            sp.wait_ge(sent, 1 + HALVES)
            load_slots(0, 0)
            load_slots(1, 1)
            with sp.Fori(0, EXPERTS // 2 - 1) as m:
                for j in range(2):
                    sp.wait_ge(et_done, 1 + 2 * m + j + 1)
                    load_slots(j, 2 * m + 2 + j)
                for j in range(2):
                    sp.wait_ge(down_done, 1 + 2 * m + j + 1)
                    load_expert(j, 2 * m + 2 + j)
                    sp.wait_ge(ye_ready, 1 + 2 * m + j + 1)
                    store_expert(j, 2 * m + j)
            for j in range(2):
                sp.wait_ge(ye_ready, 1 + EXPERTS - 1 + j)
                store_expert(j, EXPERTS - 2 + j)
            for t in range(PAIRS):
                sp.wait_ge(res_ready, t + 1)
                sp.dma_start(out[t * PT:(t + 1) * PT, :], res[:, t, :]).then_inc(out_done, 16)
            sp.wait_ge(out_done, 16 * PAIRS)

        @block.tensor
        def _(pe):
            mm = nc.tensor.matmul

            def conv(g, p):
                pe.wait_ge(ld_x[p], 16 * (g + 1))
                if p == 0:
                    pe.wait_ge(h2_ready, 1 + PH * g)
                    pe.wait_ge(before_read, 1 + PH * g)
                    pe.wait_ge(y2T_ready, 1 + PH * g)
                    pe.wait_ge(lg_ready, 1 + PH * g)
                if p >= 2:
                    pe.wait_ge(h_ready, 1 + PH * g + p - 1)
                for c in range(KC):
                    last = mm(ps[0:PT, 6 + p % 2, 0:D], xp[:, p, c, :], convw[:, c, :], start=(c == 0), stop=(c == KC - 1))
                last.then_inc(conv_done, 1)

            def transpose_y(g, p):
                pe.wait_ge(y_ready, 1 + PH * g + p + 1)
                if p == 0:
                    pe.wait_ge(sm_ready, 1 + PH * g)
                if p >= 2:
                    pe.wait_ge(yT_ready, 1 + PH * g + p - 1)
                for c in range(2):
                    last = nc.tensor.transpose(ps[0:CK, p % 2, c * PT:(c + 1) * PT], y[:, p % 2, c * CK:(c + 1) * CK], ident[0:PT, 0:PT])
                last.then_inc(yt_done, 1)

            def values(g, p):
                pe.wait_ge(yT_ready, 1 + PH * g + p + 1)
                if p == 0:
                    pe.wait_ge(pta_ready, 1 + PH * g)
                    pe.wait_ge(ptd_ready, 1 + PH * g)
                    pe.wait_ge(z_ready, 1 + PH * g)
                if p >= 2:
                    pe.wait_ge(v_ready, 1 + PH * g + p - 1)
                for j in range(2):
                    for c in range(2):
                        last = mm(ps[:, 2 + 2 * (p % 2) + j, 0:384], yT[:, c, p, :], wv[:, c, 384 * j:384 * (j + 1)], start=(c == 0), stop=(c == 1))
                last.then_inc(v_done, 1)

            def queries_keys(g):
                pe.wait_ge(yT_ready, 1 + PH * g + PH)
                pe.wait_ge(v_ready, 1 + PH * g + PH)
                for n in range(2 * HP):
                    w, ready, hp = (wk, k_ready, n // 2) if n % 2 else (wq, q_ready, n // 2)
                    if n >= 6:
                        pe.wait_ge(ready, 1 + HP * g + hp - 2)
                    for c in range(2):
                        last = mm(ps[:, n % 6, 0:PH * PT].rearrange("p (s t) -> p s t", t=TOK), w[:, c, 128 * hp:128 * (hp + 1)],
                                  yT[:, c].rearrange("p a (i s) -> p (a i) s", i=2)[:, :, 0:TOK], start=(c == 0), stop=(c == 1))
                    last.then_inc(qk_done, 1)

            def scores(g, p):
                if p == 0:
                    pe.wait_ge(q_ready, 1 + HP * g + HP)
                    pe.wait_ge(k_ready, 1 + HP * g + HP)
                else:
                    pe.wait_ge(sm_ready, 1 + PH * g + p)
                for hp in range(HP):
                    for i in range(2):
                        last = mm(ps[SLOT * i:SLOT * (i + 1), hp // 3, (hp % 3) * PT:(hp % 3 + 1) * PT], qT[:, hp, p, i, :],
                                  kB[:, hp, p, i].rearrange("p a t -> p (a t)"), start=True, stop=True)
                last.then_inc(s_done, 1)

            def transpose_p(g, p):
                pe.wait_ge(p_ready, 1 + PH * g + p + 1)
                if p >= 1:
                    pe.wait_ge(pta_ready, 1 + PH * g + p)
                    pe.wait_ge(ptd_ready, 1 + PH * g + p)
                for hp in range(HP):
                    last = nc.tensor.transpose(ps[:, 2 + hp // 3, (hp % 3) * 128:(hp % 3 + 1) * 128],
                                               prob[:, p % 2, 2 * hp:2 * hp + 2].rearrange("p a t -> p (a t)"), ident[:])
                last.then_inc(pt_done, 1)

            def outputs(g, p):
                pe.wait_ge(pta_ready, 1 + PH * g + p + 1)
                pe.wait_ge(ptd_ready, 1 + PH * g + p + 1)
                if p >= 1:
                    pe.wait_ge(z_ready, 1 + PH * g + p)
                for hp in range(HP):
                    for a in range(2):
                        hd = 2 * hp + a
                        last = mm(ps[DH * a:DH * (a + 1), 4 + hp // 3, (hp % 3) * PT:(hp % 3 + 1) * PT],
                                  v[:, p, DH * hd:DH * (hd + 1)], probT[:, hd].rearrange("p i t -> p (i t)"), start=True, stop=True)
                last.then_inc(z_done, 1)

            def project(g, p):
                pe.wait_ge(z_ready, 1 + PH * g + p + 1)
                if p >= 1:
                    pe.wait_ge(h2_ready, 1 + PH * g + p)
                if p >= 2:
                    pe.wait_ge(before_read, 1 + PH * g + p - 1)
                for c in range(HP):
                    last = mm(ps[0:PT, 6, 0:D], zT[:, p % 2, c, :], wo[:, c, :], start=(c == 0), stop=(c == HP - 1))
                last.then_inc(wo_done, 1)

            def transpose_y2(g, p):
                pe.wait_ge(y2_ready, 1 + PH * g + p + 1)
                if p >= 1:
                    pe.wait_ge(lg_ready, 1 + PH * g + p)
                for c in range(2):
                    last = nc.tensor.transpose(ps[0:CK, 7, c * PT:(c + 1) * PT], y2[:, p, c * CK:(c + 1) * CK], ident[0:PT, 0:PT])
                last.then_inc(y2t_done, 1)

            def logits(g, p):
                pe.wait_ge(y2T_ready, 1 + PH * g + p + 1)
                for c in range(2):
                    last = mm(ps[0:PT, 7, 256:256 + EXPERTS], y2T[:, c, :], gatew[:, c, :], start=(c == 0), stop=(c == 1))
                last.then_inc(lg_done, 1)

            def count_before(g, p):
                pe.wait_ge(both_ready, 1 + PH * g + p + 1)
                pe.wait_ge(seen_ready, 1 + PH * g + p)
                pe.wait_ge(h2_ready, 1 + PH * g + min(p + 2, PH))
                mm(ps[0:PT, 6, 256:256 + EXPERTS], earlier[:], both[:, p % 2, :], start=True, stop=False)
                mm(ps[0:PT, 6, 256:256 + EXPERTS], ones[:], seen[:], start=False, stop=True).then_inc(before_done, 1)

            pe.wait_ge(ld_conv, 16)
            pe.wait_ge(ld_const, 16 * CONST_LOADS)
            pe.wait_ge(sets, 2)
            with pe.Fori(0, HALVES) as g:
                for p in range(PH + 2):
                    if p < PH:
                        conv(g, p)
                    if p == 0:
                        pe.wait_ge(ld_qkv, 48)
                    if p >= 2:
                        values(g, p - 2)
                    if 1 <= p <= PH:
                        transpose_y(g, p - 1)
                queries_keys(g)
                pe.wait_ge(ld_wo, 16)
                for s in range(-2, PH + 3):
                    if 0 <= s < PH:
                        transpose_p(g, s)
                    if 0 <= s - 3 < PH:
                        count_before(g, s - 3)
                    if 0 <= s + 2 < PH:
                        scores(g, s + 2)
                    if 0 <= s - 2 < PH:
                        transpose_y2(g, s - 2)
                    if 0 <= s < PH:
                        outputs(g, s)
                    if 0 <= s - 2 < PH:
                        logits(g, s - 2)
                    if 0 <= s - 1 < PH:
                        project(g, s - 1)

            def transpose_x(m, j):
                pe.wait_ge(ld_e[j], 16 * (m + 1))
                pe.wait_ge(zeT_ready, 1 + 2 * m)
                for c in range(2):
                    for r in range(2):
                        last = nc.tensor.transpose(ps[0:CK, j, c * EC + r * EROWS:c * EC + (r + 1) * EROWS],
                                                   xe[0:EROWS, j, r, c * CK:(c + 1) * CK], ident[0:EROWS, 0:EROWS])
                last.then_inc(et_done, 1)

            def gate_up(m, j):
                pe.wait_ge(zeT_ready, 1 + 2 * m + j + 1)
                pe.wait_ge(ld_w[j], 32 * (m + 1))
                for jt in range(JT):
                    n = JT * j + jt
                    pe.wait_ge(hT_ready, 1 + 2 * JT * m + max(0, n - 3))
                    for part_ in range(2):
                        for c in range(2):
                            at = c * W13 + part_ * HID + 128 * jt
                            last = mm(ps[:, 2 + n % 4, part_ * EC:(part_ + 1) * EC], w13s[:, j, at:at + 128], zeT[:, j, c, :],
                                      start=(c == 0), stop=(c == 1))
                    last.then_inc(gu_done, 1)

            def down(m, j):
                pe.wait_ge(hT_ready, 1 + 2 * JT * m + JT * (j + 1))
                pe.wait_ge(ye_ready, 1 + 2 * m)
                for r in range(2):
                    for jt in range(JT):
                        last = mm(ps[0:EROWS, 6 + j, r * D:(r + 1) * D], hT[:, j, jt, r * EROWS:(r + 1) * EROWS], w2s[:, j, jt, :],
                                  start=(jt == 0), stop=(jt == JT - 1))
                last.then_inc(down_done, 1)

            pe.wait_ge(before_read, 1 + PAIRS)
            pe.wait_ge(lg_ready, 1 + PAIRS)
            with pe.Fori(0, EXPERTS // 2) as m:
                transpose_x(m, 0)
                transpose_x(m, 1)
                gate_up(m, 0)
                gate_up(m, 1)
                down(m, 0)
                down(m, 1)

        @block.scalar
        def _(act):
            A = nc.scalar.activation
            for dst, src in ((ident, eye), (posb, pos), (convb, conv_b), (bq, b_q), (bk, b_k), (bv, b_v), (bo, b_o),
                             (gatew, gate), (mask, causal), (earlier, before), (eno, expert_no)):
                act.dma_start(dst[:], src).then_inc(ld_const, 16)
            act.wait_ge(ld_const, 16 * CONST_LOADS)
            act.wait_ge(sets, 2)

            def bank_tokens(b):
                return ps[:, b, 0:PH * PT].rearrange("p (s t) -> p s t", t=TOK)

            with act.Fori(0, HALVES) as g:
                for p in range(PH + 1):
                    if p < PH:
                        act.wait_ge(yt_done, 1 + PH * g + p + 1)
                        A(yT[:, :, p, :].rearrange("q c (i s) -> q c i s", i=2)[:, :, :, 0:TOK],
                          ps[0:CK, p % 2, 0:2 * PT].rearrange("q (c i t) -> q c i t", c=2, i=2), ACT.Copy).then_inc(yT_ready, 1)
                    if p >= 1:
                        q = p - 1
                        act.wait_ge(v_done, 1 + PH * g + q + 1)
                        A(v[:, q, :].rearrange("r (j n) -> r j n", j=2), ps[:, 2 + 2 * (q % 2):4 + 2 * (q % 2), 0:384], ACT.Copy).then_inc(v_ready, 1)
                for hp in range(HP):
                    act.wait_ge(qk_done, 1 + 2 * HP * g + 2 * hp + 1)
                    A(qT[:, hp].rearrange("q a i s -> q (a i) s")[:, :, 0:TOK], bank_tokens(2 * hp % 6), ACT.Identity,
                      bias=bq[:, hp:hp + 1]).then_inc(q_ready, 1)
                for s in range(-2, PH + 3):
                    if 0 <= s < PH:
                        act.wait_ge(pt_done, 1 + PH * g + s + 1)
                        if s >= 1:
                            act.wait_ge(z_done, 1 + PH * g + s)
                        for a in range(2):
                            last = A(probT[SLOT:SLOT + TOK, a::2, 1, :].rearrange("k (b h) t -> k b h t", b=2),
                                     ps[SLOT * a:SLOT * a + TOK, 2:4, 0:384].rearrange("k b (h q) -> k b h q", q=128)[:, :, :, SLOT:SLOT + TOK], ACT.Copy)
                        last.then_inc(pta_ready, 1)
                    if 0 <= s - 2 < PH:
                        act.wait_ge(y2t_done, 1 + PH * g + s - 1)
                        if s > 2:
                            act.wait_ge(lg_done, 1 + PH * g + s - 2)
                        A(y2T[:], ps[0:CK, 7, 0:2 * PT].rearrange("q (c t) -> q c t", c=2), ACT.Copy).then_inc(y2T_ready, 1)
                    if 0 <= s + 2 < PH:
                        p = s + 2
                        act.wait_ge(sx_ready, 1 + PH * g + p + 1)
                        act.wait_ge(pt_done, 1 + PH * g + max(p - 1, 0))
                        A(prob[:, p % 2, :, 0:TOK], sx[:, p % 2], ACT.Exp).then_inc(exp_ready, 1)
                    if 0 <= s - 2 < PH:
                        p = s - 2
                        act.wait_ge(gap_ready, 1 + PH * g + p + 1)
                        act.wait_ge(base_ready, 1 + PH * g + max(p - 1, 0))
                        A(ratio[:, p % 2:p % 2 + 1], gap[:, p % 2:p % 2 + 1], ACT.Exp).then_inc(ratio_ready, 1)
                    if 0 <= s - 1 < PH:
                        p = s - 1
                        act.wait_ge(y2_ready, 1 + PH * g + p + 1)
                        act.wait_ge(rrms_ready, 1 + PH * g + p)
                        A(sq[:], y2[:, p, :], ACT.Square, scale=2.0, accum_out=ssq[:, p % 2:p % 2 + 1]).then_inc(ssq_ready, 1)

            with act.Fori(0, EXPERTS // 2) as m:
                for j in range(2):
                    act.wait_ge(et_done, 1 + 2 * m + j + 1)
                    act.wait_ge(ld_w[j], 32 * (m + 1))
                    act.wait_ge(gu_done, 1 + 2 * JT * m)
                    for c in range(2):
                        last = A(zeT[:, j, c, :], ps[0:CK, j, c * EC:(c + 1) * EC], ACT.Copy, scale=w13s[:, j, 2 * W13 + c:2 * W13 + c + 1])
                    last.then_inc(zeT_ready, 1)
                for j in range(2):
                    for jt in range(JT):
                        n = JT * j + jt
                        act.wait_ge(gu_done, 1 + 2 * JT * m + n + 1)
                        act.wait_ge(hT_ready, 1 + 2 * JT * m + max(0, n - 3))
                        A(sg[:, n % 4, :], ps[:, 2 + n % 4, 0:EC], ACT.Silu).then_inc(sg_ready, 1)
                for j in range(2):
                    act.wait_ge(down_done, 1 + 2 * m + j + 1)
                    act.wait_ge(stored[j], 16 + 16 * m)
                    A(ye[0:EROWS, j], ps[0:EROWS, 6 + j, 0:2 * D].rearrange("q (r d) -> q r d", r=2), ACT.Copy).then_inc(ye_ready, 1)

        @block.gpsimd
        def _(pool):
            P = nc.gpsimd
            P.memset(zeros[:], 0.0).then_inc(cleared, 1)
            P.memset(qT[:], 0.0)
            P.memset(yT[:], 0.0)
            P.memset(prob[:], 0.0)
            P.memset(ones[:], 1.0)
            P.memset(seen[:], 0.0)
            P.memset(mhalf[:], -0.5).then_inc(sets, 1)
            P.memset(ye[:], 0.0)
            P.memset(got[:], 0.0).then_inc(pool_seq, 1)
            pool.wait_ge(pool_seq, 1)
            pool.wait_ge(ld_const, 16 * CONST_LOADS)
            SEQ = 3 * PH
            with pool.Fori(0, HALVES) as g:
                n = 1

                def power(out_, in_, scale, eps, want):
                    nonlocal n
                    tmp = {0: ve, 1: ve2, 2: msq}[want[0]]
                    a = want[1]
                    P.tensor_scalar(tmp[:, a:a + 1], in_, scale, eps, ALU.mult, ALU.add).then_inc(pool_seq, 1)
                    n += 1
                    pool.wait_ge(pool_seq, SEQ * g + n)
                    return P.tensor_tensor(out_, tmp[:, a:a + 1], mhalf[:], ALU.pow)

                for p in range(PH):
                    a = p % 2
                    pool.wait_ge(mv_ready, 1 + PH * g + p + 1)
                    pool.sem_inc(held, 1)
                    power(rstd[:, a:a + 1], mv[:, a, 1:2], 1.0, LN_EPS, (0, a)).then_inc(rstd_ready, 1)
                    pool.wait_ge(h_ready, 1 + PH * g + p + 1)
                    P.tensor_tensor(hb[:, p, :], h[:, p, :], bo[:], ALU.add).then_inc(hb_ready, 1)
                for s in range(1, PH + 3):
                    if 0 <= s - 2 < PH:
                        p = s - 2
                        pool.wait_ge(ssq_ready, 1 + PH * g + p + 1)
                        pool.sem_inc(held, 1)
                        power(rrms[:, p % 2:p % 2 + 1], ssq[:, p % 2:p % 2 + 1], 1.0 / D, RMS_EPS, (2, p % 2)).then_inc(rrms_ready, 1)
                    if 0 <= s - 1 < PH:
                        p = s - 1
                        pool.wait_ge(mv2_ready, 1 + PH * g + p + 1)
                        pool.sem_inc(held, 1)
                        power(rstd2[:, p % 2:p % 2 + 1], mv2[:, p % 2, 1:2], 1.0, LN_EPS, (1, p % 2)).then_inc(rstd2_ready, 1)
                    if 0 <= s - 3 < PH:
                        p = s - 3
                        pool.wait_ge(before_done, 1 + PH * g + p + 1)
                        P.tensor_tensor(seen[:], seen[:], both[:, p % 2, :], ALU.add).then_inc(seen_ready, 1)
                        pool.wait_ge(zeroed, 64)
                        pool.wait_ge(zn_ready, 1 + PH * g + p + 1)
                        pool.wait_ge(slot_ready, 1 + PH * g + p + 1)
                        pool.sem_inc(held, 1)
                        for k in range(TOPK):
                            P.indirect_dma_start(slot_x, bass.IndirectOffsetOnAxis(slot[:, p, k:k + 1], 0), zn[:, p, :], None,
                                                 bounds_check=EXPERTS * STRIDE - 1, oob_is_err=False).then_inc(scattered[p][k], 16)
                for p in range(PH):
                    for k in range(TOPK):
                        pool.wait_ge(scattered[p][k], 16 * (g + 1))
                pool.sem_inc(sent, 1)
                assert n - 1 == SEQ

            for j in range(2):
                pool.wait_ge(stored[j], 16 + 16 * EXPERTS // 2)
            pool.wait_ge(base_ready, 1 + PAIRS)
            for t in range(PAIRS):
                for k in range(TOPK):
                    P.indirect_dma_start(got[:, t, k, :], None, slot_y, bass.IndirectOffsetOnAxis(slot_all[:, t, k:k + 1], 0),
                                         bounds_check=EXPERTS * STRIDE - 1, oob_is_err=False).then_inc(gathered[t], 16)

        @block.vector
        def _(dve):
            V = nc.vector
            V.memset(kB[:], 0.0)
            V.memset(probT[:], 0.0)
            dve.wait_ge(ld_const, 16 * CONST_LOADS)
            V.tensor_tensor(posb[:], posb[:], convb[:], ALU.add).then_inc(sets, 1)
            dve.wait_ge(sets, 2)
            SEQ = 17 * PH
            with dve.Fori(0, HALVES) as g:
                n = 0

                def then(ins, plain=False):
                    nonlocal n
                    n += 1
                    ins.then_inc(dve_seq, 1)
                    dve.wait_ge(dve_seq, SEQ * g + n)
                    if plain:
                        dve.sem_inc(held, 1)

                def embed(p):
                    dve.wait_ge(conv_done, 1 + PH * g + p + 1)
                    V.tensor_tensor(h[:, p, :], ps[0:PT, 6 + p % 2, 0:D], posb[:], ALU.add).then_inc(h_ready, 1)
                    dve.wait_ge(h_ready, 1 + PH * g + p + 1)
                    then(V.bn_stats(stats[:, p % 2, :], h[:, p, :]), plain=True)
                    V.bn_aggr(mv[:, p % 2, :], stats[:, p % 2, :]).then_inc(mv_ready, 1)

                def norm(p):
                    dve.wait_ge(rstd_ready, 1 + PH * g + p + 1)
                    if p >= 2:
                        dve.wait_ge(yt_done, 1 + PH * g + p - 1)
                    V.tensor_scalar(y[:, p % 2, :], h[:, p, :], mv[:, p % 2, 0:1], rstd[:, p % 2:p % 2 + 1], ALU.subtract, ALU.mult).then_inc(y_ready, 1)

                def keys(hp):
                    dve.wait_ge(qk_done, 1 + 2 * HP * g + 2 * hp + 2)
                    src = ps[:, (2 * hp + 1) % 6, 0:PH * PT].rearrange("q (s t) -> q s t", t=TOK)
                    for a in range(2):
                        rows = slice(DH * a, DH * (a + 1))
                        last = V.tensor_scalar(kB[rows, hp].rearrange("q p i a t -> q (p i) a t")[:, :, a, :], src[rows], bk[rows, hp:hp + 1], None, ALU.add)
                    last.then_inc(k_ready, 1)

                def soften(p):
                    a = p % 2
                    dve.wait_ge(s_done, 1 + PH * g + p + 1)
                    for b in range(2):
                        last = V.scalar_tensor_tensor(sm[:, a, 6 * b:6 * b + 6, :], ps[:, b, 0:3 * PT].rearrange("q (h t) -> q h t", t=TOK), DH ** -0.5,
                                                      mask[:, None, :].to_broadcast([128, 6, TOK]), ALU.mult, ALU.add)
                    last.then_inc(sm_ready, 1)
                    dve.wait_ge(sm_ready, 1 + PH * g + p + 1)
                    then(V.reduce_max(smax[:, a, :], sm[:, a], AX.X))
                    dve.wait_ge(exp_ready, 1 + PH * g + max(p - 1, 0))
                    V.tensor_tensor(sx[:, a], sm[:, a], smax[:, a, :, None].to_broadcast([128, HEADS, TOK]), ALU.subtract).then_inc(sx_ready, 1)

                def normalise(p):
                    a = p % 2
                    dve.wait_ge(exp_ready, 1 + PH * g + p + 1)
                    then(V.reduce_sum(ssum[:, a, :], prob[:, a, :, 0:TOK], AX.X))
                    then(V.reciprocal(srec[:, a, :], ssum[:, a, :]))
                    V.tensor_tensor(prob[:, a, :, 0:TOK], prob[:, a, :, 0:TOK], srec[:, a, :, None].to_broadcast([128, HEADS, TOK]), ALU.mult).then_inc(p_ready, 1)

                def transposed(p):
                    dve.wait_ge(pt_done, 1 + PH * g + p + 1)
                    dve.wait_ge(pta_ready, 1 + PH * g + p + 1)
                    for a in range(2):
                        last = V.tensor_copy(probT[0:TOK, a::2, 0, :].rearrange("k (b h) t -> k b h t", b=2),
                                             ps[SLOT * a:SLOT * a + TOK, 2:4, 0:384].rearrange("k b (h q) -> k b h q", q=128)[:, :, :, 0:TOK])
                    last.then_inc(ptd_ready, 1)

                def attended(p):
                    dve.wait_ge(z_done, 1 + PH * g + p + 1)
                    dve.wait_ge(wo_done, 1 + PH * g + max(p - 1, 0))
                    V.tensor_tensor(zT[:, p % 2].rearrange("q (b h) t -> q b h t", b=2), ps[:, 4:6, 0:3 * PT].rearrange("q b (h t) -> q b h t", t=PT),
                                    bv[:].rearrange("q (b h) -> q b h", b=2)[:, :, :, None].to_broadcast([128, 2, 3, PT]), ALU.add).then_inc(z_ready, 1)

                def residual(p):
                    dve.wait_ge(wo_done, 1 + PH * g + p + 1)
                    dve.wait_ge(hb_ready, 1 + PH * g + p + 1)
                    V.tensor_tensor(h2[:, p, :], ps[0:PT, 6, 0:D], hb[:, p, :], ALU.add).then_inc(h2_ready, 1)
                    dve.wait_ge(h2_ready, 1 + PH * g + p + 1)
                    then(V.bn_stats(stats2[:, p % 2, :], h2[:, p, :]), plain=True)
                    V.bn_aggr(mv2[:, p % 2, :], stats2[:, p % 2, :]).then_inc(mv2_ready, 1)

                def norm2(p):
                    dve.wait_ge(rstd2_ready, 1 + PH * g + p + 1)
                    V.tensor_scalar(y2[:, p, :], h2[:, p, :], mv2[:, p % 2, 0:1], rstd2[:, p % 2:p % 2 + 1], ALU.subtract, ALU.mult).then_inc(y2_ready, 1)

                def rms(p):
                    dve.wait_ge(rrms_ready, 1 + PH * g + p + 1)
                    if p == 0:
                        dve.wait_ge(sent, 1 + g)
                    V.tensor_scalar(zn[:, p, :], y2[:, p, :], rrms[:, p % 2:p % 2 + 1], 2.0, ALU.mult, ALU.mult).then_inc(zn_ready, 1)

                def choose(p):
                    a = p % 2
                    dve.wait_ge(lg_done, 1 + PH * g + p + 1)
                    V.tensor_copy(lg[:, a, :], ps[0:PT, 7, 256:256 + EXPERTS]).then_inc(lg_ready, 1)
                    dve.wait_ge(lg_ready, 1 + PH * g + p + 1)
                    dve.sem_inc(held, 1)
                    then(V.max(top[:, a, :], lg[:, a, :]))
                    dve.wait_ge(ratio_ready, 1 + PH * g + max(p - 1, 0))
                    V.tensor_tensor(gap[:, a:a + 1], top[:, a, 1:2], top[:, a, 0:1], ALU.subtract).then_inc(gap_ready, 1)
                    then(V.max_index(topi[:, a, :], top[:, a, :], lg[:, a, :]))
                    then(V.tensor_copy(chosen[:, a, :], topi[:, a, 0:TOPK]))
                    then(V.tensor_tensor(oneh[:, a], eno[:], chosen[:, a, :, None].to_broadcast([PT, TOPK, EXPERTS]), ALU.is_equal))
                    dve.wait_ge(seen_ready, 1 + PH * g + max(p - 1, 0))
                    V.tensor_tensor(both[:, a, :], oneh[:, a, 0, :], oneh[:, a, 1, :], ALU.add).then_inc(both_ready, 1)

                def place_rows(p):
                    a = p % 2
                    dve.wait_ge(before_done, 1 + PH * g + p + 1)
                    V.tensor_tensor(picked[:], oneh[:, a], ps[0:PT, 6, 256:256 + EXPERTS][:, None, :].to_broadcast([PT, TOPK, EXPERTS]), ALU.mult).then_inc(before_read, 1)
                    dve.wait_ge(before_read, 1 + PH * g + p + 1)
                    then(V.reduce_sum(place[:], picked[:], AX.X))
                    V.tensor_scalar(kept[:], place[:], float(CAP), None, ALU.is_lt)
                    V.tensor_scalar(far[:], place[:], float(CAP), FAR, ALU.is_ge, ALU.mult)
                    then(V.scalar_tensor_tensor(slotf[:], chosen[:, a, :], float(STRIDE), place[:], ALU.mult, ALU.add))
                    then(V.tensor_tensor(slotg[:], slotf[:], far[:], ALU.add))
                    V.tensor_copy(slot[:, p, :], slotg[:]).then_inc(slot_ready, 1)
                    V.tensor_copy(slot_all[:, PH * g + p, :], slotg[:])
                    dve.wait_ge(ratio_ready, 1 + PH * g + p + 1)
                    then(V.tensor_scalar(wsum[:], ratio[:, a:a + 1], 1.0, None, ALU.add))
                    then(V.reciprocal(share[:, 0:1], wsum[:]))
                    then(V.tensor_tensor(share[:, 1:2], share[:, 0:1], ratio[:, a:a + 1], ALU.mult))
                    then(V.tensor_tensor(cw[:], share[:], kept[:], ALU.mult))
                    V.tensor_copy(cw_all[:, PH * g + p, :], cw[:])
                    then(V.reduce_sum(csum[:], cw[:], AX.X))
                    V.scalar_tensor_tensor(base[:, PH * g + p, :], y2[:, p, :], csum[:], h2[:, p, :], ALU.mult, ALU.add).then_inc(base_ready, 1)

                for p in range(PH + 1):
                    if p < PH:
                        embed(p)
                    if p >= 1:
                        norm(p - 1)
                for hp in range(HP):
                    keys(hp)
                for s in range(-2, PH + 3):
                    if 0 <= s < PH:
                        transposed(s)
                    if 0 <= s + 1 < PH:
                        normalise(s + 1)
                    if 0 <= s - 3 < PH:
                        place_rows(s - 3)
                    if 0 <= s + 2 < PH:
                        soften(s + 2)
                    if 0 <= s - 2 < PH:
                        rms(s - 2)
                    if 0 <= s < PH:
                        attended(s)
                    if 0 <= s - 1 < PH:
                        residual(s - 1)
                    if 0 <= s - 2 < PH:
                        choose(s - 2)
                    if 0 <= s - 1 < PH:
                        norm2(s - 1)
                assert n == SEQ, n

            with dve.Fori(0, EXPERTS // 2) as m:
                for j in range(2):
                    dve.wait_ge(down_done, 1 + 2 * m)
                    for jt in range(JT):
                        k = JT * j + jt
                        dve.wait_ge(sg_ready, 1 + 2 * JT * m + k + 1)
                        V.tensor_tensor(hT[:, j, jt, :], sg[:, k % 4, :], ps[:, 2 + k % 4, EC:2 * EC], ALU.mult).then_inc(hT_ready, 1)

            dve.wait_ge(base_ready, 1 + PAIRS)
            for t in range(PAIRS):
                dve.wait_ge(gathered[t], 16 * TOPK)
                V.scalar_tensor_tensor(part[:, t % 2, :], got[:, t, 0, :], cw_all[:, t, 0:1], base[:, t, :], ALU.mult, ALU.add).then_inc(part_ready, 1)
                dve.wait_ge(part_ready, t + 1)
                V.scalar_tensor_tensor(res[:, t, :], got[:, t, 1, :], cw_all[:, t, 1:2], part[:, t % 2, :], ALU.mult, ALU.add).then_inc(res_ready, 1)


def kernel(x, L0_tok_conv_w, L0_tok_conv_b, L0_tok_pos_table, L0_attn_W_Q, L0_attn_b_Q, L0_attn_W_K, L0_attn_b_K,
           L0_attn_W_V, L0_attn_b_V, L0_attn_W_O, L0_attn_b_O, L0_ffn_gate_w, L0_ffn_w13, L0_ffn_w2, L0_ffn_norm_w):
    import concourse.bacc as bacc
    from concourse.bass_utils import run_bass_kernel_spmd
    A = np.asarray

    px = A(x).reshape(PAIRS, 2, CHANNELS, PER_SIDE, PATCH, PER_SIDE, PATCH).transpose(0, 2, 4, 6, 1, 3, 5)
    px = px.reshape(PAIRS, KC, 128, PT).transpose(0, 2, 1, 3)
    cell = np.arange(PER_SIDE) * GRID // PER_SIDE
    ids = (cell[:, None] * GRID + cell).reshape(-1)
    pos = A(L0_tok_pos_table)[np.concatenate([ids, ids])]

    def rows(a):
        return np.broadcast_to(A(a), (PT, D))

    def qkv(w):
        return A(w).transpose(1, 0, 2).reshape(2, CK, HEADS * DH).transpose(1, 0, 2)

    def head_bias(b):
        return A(b).reshape(HP, 128).T

    w13 = A(L0_ffn_w13).transpose(0, 2, 1).reshape(EXPERTS, 2, CK, 2 * HID).transpose(0, 2, 1, 3).reshape(EXPERTS, CK, 4 * HID)
    nw = A(L0_ffn_norm_w).reshape(EXPERTS, 2, CK).transpose(0, 2, 1)
    causal = np.zeros((128, TOK), np.float32)
    tri = np.where(np.arange(TOK)[:, None] >= np.arange(TOK), 0.0, IGNORE)
    causal[0:TOK], causal[SLOT:SLOT + TOK] = tri, tri
    arrays = {
        "patches": px,
        "conv_w": A(L0_tok_conv_w).reshape(D, KC, 128).transpose(2, 1, 0),
        "conv_b": rows(L0_tok_conv_b),
        "pos": pos,
        "w_q": qkv(L0_attn_W_Q), "w_k": qkv(L0_attn_W_K), "w_v": qkv(L0_attn_W_V),
        "w_o": A(L0_attn_W_O).reshape(HP, 128, D).transpose(1, 0, 2),
        "b_q": head_bias(L0_attn_b_Q), "b_k": head_bias(L0_attn_b_K), "b_v": head_bias(L0_attn_b_V),
        "b_o": rows(L0_attn_b_O),
        "gate": A(L0_ffn_gate_w).T.reshape(2, CK, EXPERTS).transpose(1, 0, 2),
        "w13": np.concatenate([w13, nw], axis=2),
        "w2": A(L0_ffn_w2).transpose(0, 2, 1).reshape(EXPERTS, JT, 128, D).transpose(0, 2, 1, 3),
        "eye": np.eye(128, dtype=np.float32),
        "causal": causal,
        "before": np.triu(np.ones((PT, PT), np.float32), 1).astype(mybir.dt.np(mybir.dt.bfloat16)),
        "expert_no": np.broadcast_to(np.arange(EXPERTS, dtype=np.float32), (PT, TOPK, EXPERTS)),
    }
    nc = bacc.Bacc("TRN2", target_bir_lowering=False, num_devices=1)
    feed, args = {}, []
    for name, a in arrays.items():
        feed[name] = np.ascontiguousarray(a)
        args.append(nc.dram_tensor(name, feed[name].shape, mybir.dt.from_np(feed[name].dtype), kind="ExternalInput").ap())
    out = nc.dram_tensor("out", (N, D), mybir.dt.float32, kind="ExternalOutput").ap()
    vit_block(nc, *args, out)
    got = run_bass_kernel_spmd(nc, [feed], core_ids=[0])
    return got.results[0]["out"].reshape(IMAGES, TOK, D)
```

```python
from contextlib import ExitStack

import numpy as np
import concourse.bass as bass
from concourse import mybir

IMAGES, CHANNELS, SIDE, PATCH = 16, 3, 112, 16
PER_SIDE = SIDE // PATCH
TOK = PER_SIDE * PER_SIDE
D = 192
DA, DR = 128, 64
HEADS, DH = 12, 64
QKV = HEADS * DH
HP = HEADS // 2
EXPERTS, TOPK, HID = 8, 2, 512
N = IMAGES * TOK
CAP = -(-5 * TOPK * N // (4 * EXPERTS))
GRID = 32

PT = 2 * TOK
PAIRS = IMAGES // 2
PH = 4
SLOT = 64
EVEN = TOK + 1
KC = CHANNELS * PATCH * PATCH // 128
STRIDE = 256
EROWS = (CAP + 1) // 2
EC = 2 * EROWS
JT = HID // 128
XW = D + 4
FAR = float(1 << 20)
LN_EPS, RMS_EPS = 1e-5, 1e-6
IGNORE = -100000.0


def vit_block(nc, patches, conv_w, conv_b, pos, w_qkv, w_o, b_q, b_k, b_v, b_o, gate, w13, w2,
              eye, causal, before, expert_no, token_no, blank, out):
    f32, f32r, bf16, u32 = mybir.dt.float32, mybir.dt.float32r, mybir.dt.bfloat16, mybir.dt.uint32
    ALU, ACT, AX = mybir.AluOpType, mybir.ActivationFunctionType, mybir.AxisListType

    slots = nc.dram_tensor("slots", [EXPERTS * STRIDE, XW], f32, kind="Internal").ap()

    with ExitStack() as ctx:
        def sb(name, shape, dt=f32):
            return ctx.enter_context(nc.sbuf_tensor(name, shape, dt))

        def sem(name):
            return ctx.enter_context(nc.semaphore(name))

        convw = sb("convw", [128, KC, D])
        posb = sb("posb", [PT, D])
        convb = sb("convb", [PT, D])
        raw = sb("raw", [128, 3 * 2 * QKV])
        wqkv = sb("wqkv", [128, 3, 2, 2, QKV], f32r)
        wo = sb("wo", [128, HP, D])
        bq = sb("bq", [128, HP])
        bk = sb("bk", [128, HP])
        bv = sb("bv", [128, HP])
        bo = sb("bo", [PT, D])
        gatew = sb("gatew", [D // 2, 2, EXPERTS])
        ident = sb("ident", [128, 128])
        mask = sb("mask", [128, TOK])
        earlier = sb("earlier", [PT, PT], bf16)
        ones = sb("ones", [PT, PT], bf16)
        eno = sb("eno", [PT, TOPK, EXPERTS])
        tno = sb("tno", [PT, PAIRS])
        mhalf = sb("mhalf", [PT, 1])
        xp = sb("xp", [128, PH, KC, PT])
        h = sb("h", [PT, PAIRS, D])
        y = sb("y", [PT, 2, D])
        yA = sb("yA", [128, 2, PH, 128], f32r)
        yR = sb("yR", [128, PH, 128], f32r)
        qT = sb("qT", [128, HP, PH, 2, SLOT])
        kB = sb("kB", [128, HP, PH, 2, 2, TOK])
        v = sb("v", [128, PH, QKV])
        stats = sb("stats", [PT, 2, 6])
        mv = sb("mv", [PT, 2, 2])
        ve = sb("ve", [PT, 2])
        rstd = sb("rstd", [PT, 2])
        sm = sb("sm", [128, 2, HEADS, TOK])
        prob = sb("prob", [128, 2, HEADS, SLOT])
        smax = sb("smax", [128, 2, HEADS])
        ssum = sb("ssum", [128, 2, HEADS])
        srec = sb("srec", [128, 2, HEADS])
        probT = sb("probT", [128, HEADS, 2, TOK])
        zT = sb("zT", [128, 2, HP, PT])
        bvx = zT[:, 0]
        h2 = sb("h2", [PT, PH, D])
        y2 = sb("y2", [PT, PH, D])
        y2T = sb("y2T", [D // 2, 2, PT])
        sq = sb("sq", [PT, D])
        ssq = sb("ssq", [PT, 2])
        msq = sb("msq", [PT, 2])
        rrms = sb("rrms", [PT, 2])
        stats2 = sb("stats2", [PT, 2, 6])
        mv2 = sb("mv2", [PT, 2, 2])
        ve2 = sb("ve2", [PT, 2])
        rstd2 = sb("rstd2", [PT, 2])
        row = sb("row", [PT, 2, TOPK, XW])
        top = sb("top", [PT, 2, 8])
        topi = sb("topi", [PT, 2, 8], u32)
        oneh = sb("oneh", [PT, 2, TOPK, EXPERTS])
        both = sb("both", [PT, 2, EXPERTS], bf16)
        seen = sb("seen", [PT, EXPERTS], bf16)
        gap = sb("gap", [PT, 2])
        ratio = sb("ratio", [PT, 2])
        picked = sb("picked", [PT, TOPK, EXPERTS])
        place = sb("place", [PT, TOPK])
        kept = sb("kept", [PT, TOPK])
        far = sb("far", [PT, TOPK])
        slotf = sb("slotf", [PT, TOPK])
        slotg = sb("slotg", [PT, TOPK])
        slot = sb("slot", [PT, PH, TOPK], u32)
        wsum = sb("wsum", [PT, 1])
        share = sb("share", [PT, TOPK])
        csum = sb("csum", [PT, 1])
        cw = sb("cw", [PT, TOPK])
        base = sb("base", [PT, 2, D])
        W13 = 2 * HID
        RAW = 2 * W13 + 2
        raw13 = [raw[:, j * RAW:(j + 1) * RAW] for j in range(2)]
        wsp = sb("wsp", [128, 2, 2, 2, W13], f32r)
        meta = sb("meta", [EROWS, EXPERTS, 2, 2])
        cwe = sb("cwe", [EROWS, 2, 2])
        toke = sb("toke", [EROWS, 2, 2], u32)
        zeA = sb("zeA", [128, 2, 2, EC], f32r)
        zeR = sb("zeR", [128, 2, EC], f32r)
        xflat = xp[:].rearrange("p a c t -> p (a c t)")
        w2s = xflat[:, 0:2 * JT * D].rearrange("p (j t d) -> p j t d", j=2, t=JT)
        xe = xflat[:, 2 * JT * D:2 * JT * D + 4 * XW].rearrange("p (j r d) -> p j r d", j=2, r=2)
        vflat = v[:].rearrange("p a n -> p (a n)")
        hT = vflat[:, 0:2 * JT * EC].rearrange("p (j t n) -> p j t n", j=2, t=JT)
        sg = vflat[:, 2 * JT * EC:2 * JT * EC + 4 * EC].rearrange("p (k n) -> p k n", k=4)
        ye = qT[:].rearrange("p a b c d -> p (a b c d)")[:, 0:4 * D].rearrange("p (j r d) -> p j r d", j=2, r=2)

        ps = ctx.enter_context(nc.psum_tensor("ps", [128, 8, 512], f32))

        ld_eye, ld_pos, ld_bias, ld_const, ld_wo, zeroed = (sem(x) for x in ("ld_eye", "ld_pos", "ld_bias", "ld_const", "ld_wo", "zeroed"))
        ld_conv = [sem(f"ld_conv{j}") for j in range(2)]
        ld_x = [sem(f"ld_x{p}") for p in range(PH)]
        ld_qkv = [sem(f"ld_qkv{w}") for w in range(3)]
        ld_w = [sem(f"ld_w{j}") for j in range(2)]
        ld_d = [sem(f"ld_d{j}") for j in range(2)]
        ld_e = [sem(f"ld_e{j}") for j in range(2)]
        y_zeroed, all_zeroed, kb_zeroed = sem("y_zeroed"), sem("all_zeroed"), sem("kb_zeroed")
        conv_done, yt_done, v_done, qk_done = (sem(x) for x in ("conv_done", "yt_done", "v_done", "qk_done"))
        s_done, pt_done, z_done, wo_done = (sem(x) for x in ("s_done", "pt_done", "z_done", "wo_done"))
        y2t_done, lg_done, before_done = (sem(x) for x in ("y2t_done", "lg_done", "before_done"))
        h_ready, mv_ready, rstd_ready, y_ready, hb_ready = (sem(x) for x in ("h_ready", "mv_ready", "rstd_ready", "y_ready", "hb_ready"))
        yhi_ready, ylo_ready, v_ready, q_ready = (sem(x) for x in ("yhi_ready", "ylo_ready", "v_ready", "q_ready"))
        k0_ready, k1_ready, whi_ready, wlo_ready = (sem(x) for x in ("k0_ready", "k1_ready", "whi_ready", "wlo_ready"))
        sm_ready, smax_ready, sx_ready, exp_ready, p_ready = (sem(x) for x in ("sm_ready", "smax_ready", "sx_ready", "exp_ready", "p_ready"))
        pt_ready, z_ready = sem("pt_ready"), sem("z_ready")
        h2_ready, mv2_ready, rstd2_ready, y2_ready = (sem(x) for x in ("h2_ready", "mv2_ready", "rstd2_ready", "y2_ready"))
        y2T_ready, ssq_ready, rrms_ready, row_ready, cw_ready = (sem(x) for x in ("y2T_ready", "ssq_ready", "rrms_ready", "row_ready", "cw_ready"))
        bvx_ready, bo_done, bo_ready = (sem(x) for x in ("bvx_ready", "bo_done", "bo_ready"))
        both_ready, gap_ready, ratio_ready = (sem(x) for x in ("both_ready", "gap_ready", "ratio_ready"))
        before_read, slot_ready, seen_ready, base_ready = (sem(x) for x in ("before_read", "slot_ready", "seen_ready", "base_ready"))
        scattered = [[sem(f"scattered{a}{k}") for k in range(TOPK)] for a in range(2)]
        based = [sem(f"based{a}") for a in range(2)]
        dve_seq, pool_seq = sem("dve_seq"), sem("pool_seq")
        et_done, gu_done, down_done = sem("et_done"), sem("gu_done"), sem("down_done")
        zehi_ready, zelo_ready, sg_ready, hT_ready = (sem(x) for x in ("zehi_ready", "zelo_ready", "sg_ready", "hT_ready"))
        ehi_ready, elo_ready, meta_ready, toke_ready, ye_ready = (sem(x) for x in ("ehi_ready", "elo_ready", "meta_ready", "toke_ready", "ye_ready"))
        added = [[sem(f"added{j}{r}") for r in range(2)] for j in range(2)]
        flushed = sem("flushed")
        held = sem("held")
        BIAS = 2
        counted = (et_done, gu_done, down_done, zehi_ready, zelo_ready, sg_ready, hT_ready, ehi_ready, elo_ready,
                   meta_ready, toke_ready, ye_ready, flushed)

        def at(per_expert, m, c, more=0):
            return 2 * per_expert * m + (BIAS + per_expert * c + more)

        CONST_LOADS = 8
        CA = KC // 2
        FIRST, LAST = range(PH), range(PH, PAIRS)
        block = ctx.enter_context(nc.Block())

        def conv_bank(p):
            return PH + p if p < PH else 6

        def yt_bank(p):
            return p if p < PH else 7

        STEPS = range(-2, PAIRS + 2)

        def in_pairs(p):
            return 0 <= p < PAIRS

        def embedded(s):
            return (s + PH + 2,) if s < 2 else ()

        @block.sync
        def _(sp):
            def load_w13(e, j):
                sp.dma_start(raw13[j], w13[e]).then_inc(ld_w[j], 16)

            def load_w2(e, j):
                sp.dma_start(w2s[:, j], w2[e]).then_inc(ld_d[j], 16)

            def load_slots(e, j):
                sp.dma_start(xe[:, j], slots[bass.ds(e * STRIDE, STRIDE), :].rearrange("(p two) d -> p two d", two=2)).then_inc(ld_e[j], 16)

            sp.dma_start(convw[:, 0:CA], conv_w[:, 0:CA]).then_inc(ld_conv[0], 16)
            sp.dma_start(xp[:, 0], patches[0]).then_inc(ld_x[0], 16)
            sp.dma_start(convw[:, CA:KC], conv_w[:, CA:KC]).then_inc(ld_conv[1], 16)
            for p in FIRST[1:]:
                sp.dma_start(xp[:, p], patches[p]).then_inc(ld_x[p], 16)
            for w in range(3):
                sp.dma_start(raw[:, w * 2 * QKV:(w + 1) * 2 * QKV], w_qkv[w]).then_inc(ld_qkv[w], 16)
            sp.dma_start(wo[:], w_o).then_inc(ld_wo, 16)
            for c in counted:
                sp.sem_inc(c, BIAS)
            for p in FIRST:
                sp.wait_ge(conv_done, p + 1)
                sp.dma_start(xp[:, p], patches[PH + p]).then_inc(ld_x[p], 16)
            for e in range(EXPERTS):
                sp.dma_start(slots[e * STRIDE:(e + 1) * STRIDE, :], blank).then_inc(zeroed, 16)
            sp.dma_start(out[N:N + STRIDE, :], blank[:, 0:D]).then_inc(zeroed, 16)
            sp.wait_ge(wlo_ready, 3)
            for j in range(2):
                load_w13(j, j)
            sp.wait_ge(conv_done, PAIRS)
            for j in range(2):
                load_w2(j, j)
            for p in range(PAIRS):
                sp.wait_ge(base_ready, p + 1)
                sp.dma_start(out[p * PT:(p + 1) * PT, :], base[:, p % 2, :]).then_inc(based[p % 2], 16)
            for a in range(2):
                for k in range(TOPK):
                    sp.wait_ge(scattered[a][k], 16 * PAIRS // 2)
            load_slots(0, 0)
            load_slots(1, 1)

            def reload(m, c, j):
                sp.wait_ge(elo_ready, at(1, m, c + 1))
                sp.wait_ge(zelo_ready, at(1, m, c + 1))
                load_w13(2 * m + c + 2, j)
                sp.wait_ge(et_done, at(1, m, c + 1))
                sp.wait_ge(meta_ready, at(1, m, c + 1))
                load_slots(2 * m + c + 2, j)

            def reload_w2(m, c, j):
                sp.wait_ge(down_done, at(1, m, c + 1))
                load_w2(2 * m + c + 2, j)

            reload(0, 0, 0)
            reload(0, 1, 1)
            with sp.Fori(0, EXPERTS // 2 - 2) as m:
                for j in range(2):
                    reload(m, 2 + j, j)
                    reload_w2(m, j, j)
            for j in range(2):
                reload_w2(EXPERTS // 2 - 2, j, j)

        @block.tensor
        def _(pe):
            mm = nc.tensor.matmul

            def conv(p):
                pe.wait_ge(ld_x[p % PH], 16 * (1 + p // PH))
                if p >= PH:
                    pe.wait_ge(h_ready, p)
                if p == PAIRS - 1:
                    pe.wait_ge(h2_ready, 1)
                for c in range(KC):
                    if p == 0 and c == CA:
                        pe.wait_ge(ld_conv[1], 16)
                    last = mm(ps[0:PT, conv_bank(p), 0:D], xp[:, p % PH, c, :], convw[:, c, :], start=(c == 0), stop=(c == KC - 1))
                last.then_inc(conv_done, 1)

            def transpose_y(p):
                bank = yt_bank(p)
                pe.wait_ge(y_ready, p + 1)
                if p == PH:
                    pe.wait_ge(h_ready, PH)
                    pe.wait_ge(bo_ready, 1)
                elif p == PH + 1:
                    pe.wait_ge(ylo_ready, p)
                elif p == PH + 2:
                    pe.wait_ge(both_ready, 1)
                elif p > PH:
                    pe.wait_ge(before_read, 1)
                nc.tensor.transpose(ps[:, bank, 0:PT], y[:, p % 2, 0:DA], ident[0:PT, 0:PT])
                nc.tensor.transpose(ps[0:DR, bank, 128:128 + PT], y[:, p % 2, DA:D], ident[0:PT, 0:PT]).then_inc(yt_done, 1)

            def values(p):
                pe.wait_ge(wlo_ready, 3)
                pe.wait_ge(ylo_ready, p + 1)
                if p >= 1:
                    pe.wait_ge(pt_ready, p)
                q = p % PH
                for j in range(2):
                    c = slice(384 * j, 384 * (j + 1))
                    o = ps[:, 2 + j, 0:384]
                    mm(o, yA[:, 0, q, :], wqkv[:, 2, 0, 0, c], start=True, stop=False)
                    mm(o, yA[:, 0, q, :], wqkv[:, 2, 1, 0, c], start=False, stop=False)
                    mm(o, yA[:, 1, q, :], wqkv[:, 2, 0, 0, c], start=False, stop=False)
                    mm(o, yR[:, q, :], wqkv[:, 2, 0, 1, c], start=False, stop=False)
                    last = mm(o, yR[:, q, :], wqkv[:, 2, 1, 1, c], start=False, stop=True)
                last.then_inc(v_done, 1)

            def queries_keys(half):
                if half:
                    pe.wait_ge(sm_ready, PH)
                    pe.wait_ge(z_ready, PH - 1)
                pe.wait_ge(ylo_ready, PH * (half + 1))
                for n in range(2 * HP):
                    w, hp = n % 2, n // 2
                    if not half and n < 2:
                        pe.wait_ge(wlo_ready, n + 1)
                    if n >= 4:
                        if w:
                            pe.wait_ge(k0_ready, HP * half + hp - 1)
                            pe.wait_ge(k1_ready, HP * half + hp - 1)
                        else:
                            pe.wait_ge(q_ready, HP * half + hp - 1)
                    c = slice(128 * hp, 128 * (hp + 1))
                    o = ps[:, (0, 1, 4, 5)[n % 4], 0:2 * PH * EVEN].rearrange("p (s t) -> p s t", t=EVEN)

                    def tokens(t):
                        return t.rearrange("p a (i s) -> p (a i) s", i=2)[:, :, 0:EVEN]
                    mm(o, wqkv[:, w, 0, 0, c], tokens(yA[:, 0]), start=True, stop=False)
                    mm(o, wqkv[:, w, 0, 0, c], tokens(yA[:, 1]), start=False, stop=False)
                    mm(o, wqkv[:, w, 1, 0, c], tokens(yA[:, 0]), start=False, stop=False)
                    mm(o, wqkv[:, w, 0, 1, c], tokens(yR[:]), start=False, stop=False)
                    mm(o, wqkv[:, w, 1, 1, c], tokens(yR[:]), start=False, stop=True).then_inc(qk_done, 1)

            def scores(p):
                if p >= 1:
                    pe.wait_ge(sm_ready, p)
                for hp in range(HP):
                    if p % PH == 0 and hp in (0, HP - 1):
                        for ready in (q_ready, k0_ready, k1_ready):
                            pe.wait_ge(ready, HP * (p // PH) + (HP - 1 if hp == 0 else HP))
                    for i in range(2):
                        last = mm(ps[SLOT * i:SLOT * (i + 1), hp // 3, (hp % 3) * PT:(hp % 3 + 1) * PT], qT[:, hp, p % PH, i, :],
                                  kB[:, hp, p % PH, i].rearrange("p a t -> p (a t)"), start=True, stop=True)
                last.then_inc(s_done, 1)

            def transpose_p(p):
                pe.wait_ge(p_ready, p + 1)
                pe.wait_ge(v_ready, p + 1)
                for hp in range(HP):
                    last = nc.tensor.transpose(ps[:, 2 + hp // 3, (hp % 3) * 128:(hp % 3 + 1) * 128],
                                               prob[:, p % 2, 2 * hp:2 * hp + 2].rearrange("p a t -> p (a t)"), ident[:])
                last.then_inc(pt_done, 1)

            def outputs(p):
                pe.wait_ge(pt_ready, p + 1)
                if p >= 1:
                    pe.wait_ge(z_ready, p)
                for hp in range(HP):
                    for a in range(2):
                        hd = 2 * hp + a
                        last = mm(ps[DH * a:DH * (a + 1), 4 + hp // 3, (hp % 3) * PT:(hp % 3 + 1) * PT],
                                  v[:, p % PH, DH * hd:DH * (hd + 1)], probT[:, hd].rearrange("p i t -> p (i t)"), start=True, stop=True)
                last.then_inc(z_done, 1)

            def project(p):
                pe.wait_ge(z_ready, p + 1)
                if p >= 1:
                    pe.wait_ge(h2_ready, p)
                pe.wait_ge(h_ready, PAIRS - 1 if p == 0 else PAIRS)
                for c in range(HP):
                    last = mm(ps[0:PT, 6, 0:D], zT[:, p % 2, c, :], wo[:, c, :], start=(c == 0), stop=(c == HP - 1))
                last.then_inc(wo_done, 1)

            def transpose_y2(p):
                pe.wait_ge(y2_ready, p + 1)
                pe.wait_ge(ylo_ready, PH + 2 if p == 0 else PAIRS)
                if p >= 1:
                    pe.wait_ge(before_read, p)
                for c in range(2):
                    last = nc.tensor.transpose(ps[0:D // 2, 7, c * PT:(c + 1) * PT], y2[:, p % PH, c * D // 2:(c + 1) * D // 2], ident[0:PT, 0:PT])
                last.then_inc(y2t_done, 1)

            def logits(p):
                pe.wait_ge(y2T_ready, p + 1)
                for c in range(2):
                    last = mm(ps[0:PT, 7, 256:256 + EXPERTS], y2T[:, c, :], gatew[:, c, :], start=(c == 0), stop=(c == 1))
                last.then_inc(lg_done, 1)

            def count_before(p):
                pe.wait_ge(both_ready, p + 1)
                if p == 0:
                    pe.wait_ge(ylo_ready, PAIRS - 1)
                else:
                    pe.wait_ge(seen_ready, p)
                mm(ps[0:PT, 7, 264:264 + EXPERTS], earlier[:], both[:, p % 2, :], start=True, stop=False)
                mm(ps[0:PT, 7, 264:264 + EXPERTS], ones[:], seen[:], start=False, stop=True).then_inc(before_done, 1)

            def bias_values():
                pe.wait_ge(ld_wo, 16)
                pe.wait_ge(bvx_ready, 1)
                pe.wait_ge(h_ready, PH)
                for c in range(HP):
                    last = mm(ps[0:PT, 7, 0:D], bvx[:, c, :], wo[:, c, :], start=(c == 0), stop=(c == HP - 1))
                last.then_inc(bo_done, 1)

            pe.wait_ge(ld_conv[0], 16)
            for p in FIRST:
                conv(p)
                if p == PH - 2:
                    pe.wait_ge(ld_eye, 16)
                    transpose_y(0)
            for p in FIRST[1:]:
                transpose_y(p)
            pe.wait_ge(ld_const, 16 * CONST_LOADS)
            pe.wait_ge(all_zeroed, 1)
            queries_keys(0)
            for s in STEPS:
                if in_pairs(s):
                    transpose_p(s)
                if in_pairs(s + 2) and s != PH - 2:
                    scores(s + 2)
                if s in (0, 1):
                    transpose_y(PH + s)
                if in_pairs(s - 2):
                    logits(s - 2)
                if in_pairs(s - 1):
                    project(s - 1)
                if in_pairs(s + 1):
                    values(s + 1)
                if s == -1:
                    bias_values()
                if s == PH - 2:
                    transpose_y(PAIRS - 2)
                if in_pairs(s):
                    outputs(s)
                if in_pairs(s - 2):
                    count_before(s - 2)
                if s == PH - 2:
                    transpose_y(PAIRS - 1)
                for p in embedded(s):
                    conv(p)
                if in_pairs(s - 1):
                    transpose_y2(s - 1)
                if s == PH - 2:
                    queries_keys(1)
                    scores(s + 2)

            def transpose_x(e, j):
                for r in range(2):
                    c = r * EROWS
                    nc.tensor.transpose(ps[:, j, c:c + EROWS], xe[0:EROWS, j, r, 0:DA], ident[0:EROWS, 0:EROWS])
                    last = nc.tensor.transpose(ps[0:DR, j, EC + c:EC + c + EROWS], xe[0:EROWS, j, r, DA:D], ident[0:EROWS, 0:EROWS])
                last.then_inc(et_done, 1)

            def gate_up(m, c, j):
                pe.wait_ge(zelo_ready, at(1, m, c + 1))
                pe.wait_ge(elo_ready, at(1, m, c + 1))
                for jt in range(JT):
                    if c:
                        pe.wait_ge(hT_ready, at(JT, m, c, jt - 3))
                    for u in range(2):
                        o = ps[:, 2 + jt, u * EC:(u + 1) * EC]
                        w = slice(u * HID + 128 * jt, u * HID + 128 * (jt + 1))
                        mm(o, wsp[:, j, 0, 0, w], zeA[:, j, 0, :], start=True, stop=False)
                        mm(o, wsp[:, j, 0, 0, w], zeA[:, j, 1, :], start=False, stop=False)
                        mm(o, wsp[:, j, 1, 0, w], zeA[:, j, 0, :], start=False, stop=False)
                        mm(o, wsp[:, j, 0, 1, w], zeR[:, j, :], start=False, stop=False)
                        last = mm(o, wsp[:, j, 1, 1, w], zeR[:, j, :], start=False, stop=True)
                    last.then_inc(gu_done, 1)

            def down(m, c, j):
                pe.wait_ge(hT_ready, at(JT, m, c + 1))
                pe.wait_ge(ld_d[j], 16 * (m + 1))
                pe.wait_ge(ye_ready, at(1, m, c - 1))
                for r in range(2):
                    for jt in range(JT):
                        last = mm(ps[0:EROWS, 6 + j, r * D:(r + 1) * D], hT[:, j, jt, r * EROWS:(r + 1) * EROWS], w2s[:, j, jt, :],
                                  start=(jt == 0), stop=(jt == JT - 1))
                last.then_inc(down_done, 1)

            for j in range(2):
                pe.wait_ge(ld_e[j], 16)
                transpose_x(j, j)
            gate_up(0, 0, 0)
            with pe.Fori(0, EXPERTS // 2 - 1) as m:
                for j in range(2):
                    gate_up(m, 1 + j, 1 - j)
                    pe.wait_ge(ld_e[j], 16 * (m + 2))
                    pe.wait_ge(zelo_ready, at(1, m, 1 + j))
                    transpose_x(2 * m + 2 + j, j)
                    down(m, j, j)
            gate_up(EXPERTS // 2 - 1, 1, 1)
            for j in range(2):
                down(EXPERTS // 2 - 1, j, j)

        @block.scalar
        def _(act):
            A = nc.scalar.activation
            act.dma_start(bv[:], b_v).then_inc(ld_bias, 16)
            for dst, src in ((posb, pos), (convb, conv_b)):
                act.dma_start(dst[:], src).then_inc(ld_pos, 16)
            act.dma_start(ident[:], eye).then_inc(ld_eye, 16)
            for dst, src in ((bq, b_q), (bk, b_k), (mask, causal), (gatew, gate), (earlier, before), (bo, b_o), (eno, expert_no), (tno, token_no)):
                act.dma_start(dst[:], src).then_inc(ld_const, 16)

            def y_hi(p):
                act.wait_ge(yt_done, p + 1)
                q, bank = p % PH, yt_bank(p)
                A(yA[:, 0, q, :].rearrange("q (i s) -> q i s", i=2)[:, :, 0:TOK], ps[:, bank, 0:PT].rearrange("q (i t) -> q i t", i=2), ACT.Copy)
                A(yR[0:DR, q, :].rearrange("q (i s) -> q i s", i=2)[:, :, 0:TOK], ps[0:DR, bank, 128:128 + PT].rearrange("q (i t) -> q i t", i=2),
                  ACT.Copy).then_inc(yhi_ready, 1)

            def queries_keys(half, some):
                for n in some:
                    hp, w = n // 2, n % 2
                    act.wait_ge(qk_done, 2 * HP * half + n + 1)
                    o = ps[:, (0, 1, 4, 5)[n % 4], 0:2 * PH * EVEN].rearrange("p (s t) -> p s t", t=EVEN)
                    if w:
                        A(kB[0:DH, hp].rearrange("q p i a t -> q (p i) a t")[:, :, 0, :], o[0:DH, :, 0:TOK], ACT.Identity,
                          bias=bk[0:DH, hp:hp + 1]).then_inc(k0_ready, 1)
                    else:
                        A(qT[:, hp].rearrange("q a i s -> q (a i) s")[:, :, 0:TOK], o[:, :, 0:TOK], ACT.Identity,
                          bias=bq[:, hp:hp + 1]).then_inc(q_ready, 1)

            def split_qkv(w):
                act.wait_ge(ld_qkv[w], 16)
                A(wqkv[:, w, 0].rearrange("q c n -> q (c n)"), raw[:, 2 * QKV * w:2 * QKV * (w + 1)], ACT.Copy).then_inc(whi_ready, 1)

            def diagonal(p):
                act.wait_ge(pt_done, p + 1)
                if p >= 1:
                    act.wait_ge(z_done, p)
                for i in range(2):
                    for a in range(2):
                        last = A(probT[SLOT * i:SLOT * i + TOK, a::2, i, :].rearrange("k (b h) t -> k b h t", b=2),
                                 ps[SLOT * a:SLOT * a + TOK, 2:4, 0:384].rearrange("k b (h q) -> k b h q", q=128)[:, :, :, SLOT * i:SLOT * i + TOK],
                                 ACT.Copy)
                last.then_inc(pt_ready, 1)

            def weigh_second(p):
                act.wait_ge(gap_ready, p + 1)
                if p >= 2:
                    act.wait_ge(base_ready, p - 1)
                A(ratio[:, p % 2:p % 2 + 1], gap[:, p % 2:p % 2 + 1], ACT.Exp).then_inc(ratio_ready, 1)

            def exponentials(p):
                act.wait_ge(sx_ready, p + 1)
                if p >= 2:
                    act.wait_ge(pt_done, p - 1)
                A(prob[:, p % 2, :, 0:TOK], sm[:, p % 2], ACT.Exp).then_inc(exp_ready, 1)

            def values(p):
                act.wait_ge(v_done, p + 1)
                A(v[:, p % PH, :].rearrange("r (j n) -> r j n", j=2), ps[:, 2:4, 0:384], ACT.Copy).then_inc(v_ready, 1)

            def outputs(p):
                act.wait_ge(z_done, p + 1)
                if p >= 2:
                    act.wait_ge(wo_done, p - 1)
                A(zT[:, p % 2].rearrange("q (b h) t -> q b (h t)", b=2), ps[:, 4:6, 0:3 * PT], ACT.Copy).then_inc(z_ready, 1)

            def squares(p):
                act.wait_ge(y2_ready, p + 1)
                if p >= 2:
                    act.wait_ge(rrms_ready, p - 1)
                A(sq[:], y2[:, p % PH, :], ACT.Square, accum_out=ssq[:, p % 2:p % 2 + 1]).then_inc(ssq_ready, 1)

            def rows(p):
                act.wait_ge(rrms_ready, p + 1)
                if p >= 2:
                    for k in range(TOPK):
                        act.wait_ge(scattered[p % 2][k], 16 * (p // 2))
                A(row[:, p % 2, :, 0:D], y2[:, p % PH, None, :].to_broadcast([PT, TOPK, D]), ACT.Copy, scale=rrms[:, p % 2:p % 2 + 1])
                A(row[:, p % 2, :, D + 1:D + 2], tno[:, p:p + 1, None].to_broadcast([PT, TOPK, 1]), ACT.Copy).then_inc(row_ready, 1)

            def transposed_y2(p):
                act.wait_ge(y2t_done, p + 1)
                if p >= 1:
                    act.wait_ge(lg_done, p)
                A(y2T[:], ps[0:D // 2, 7, 0:2 * PT].rearrange("q (c t) -> q c t", c=2), ACT.Copy).then_inc(y2T_ready, 1)

            act.wait_ge(ld_bias, 16)
            A(bvx[:], bv[:, :, None].to_broadcast([128, HP, PT]), ACT.Copy).then_inc(bvx_ready, 1)
            act.wait_ge(y_zeroed, 1)
            y_hi(0)
            y_hi(1)
            split_qkv(0)
            y_hi(2)
            y_hi(3)
            split_qkv(1)
            act.wait_ge(ld_const, 16 * CONST_LOADS)
            act.wait_ge(all_zeroed, 1)
            act.wait_ge(kb_zeroed, 1)
            queries_keys(0, range(HP))
            split_qkv(2)
            queries_keys(0, range(HP, 2 * HP))
            for s in STEPS:
                if in_pairs(s):
                    diagonal(s)
                if s in (0, 1):
                    y_hi(PH + s)
                if in_pairs(s - 2):
                    weigh_second(s - 2)
                if in_pairs(s + 2) and s != PH - 2:
                    exponentials(s + 2)
                if in_pairs(s + 1):
                    values(s + 1)
                if s == PH - 2:
                    y_hi(PAIRS - 2)
                if in_pairs(s - 1):
                    squares(s - 1)
                    rows(s - 1)
                if in_pairs(s):
                    outputs(s)
                if s == PH - 2:
                    y_hi(PAIRS - 1)
                if in_pairs(s - 1):
                    transposed_y2(s - 1)
                if s == PH - 2:
                    queries_keys(1, range(2 * HP))
                    exponentials(s + 2)

            def split_hi(j, c):
                A(wsp[:, j, 0, c, :], raw13[j][:, c * W13:(c + 1) * W13], ACT.Copy).then_inc(ehi_ready, 1)

            def x_hi(m, c, j):
                act.wait_ge(et_done, at(1, m, c + 1))
                A(zeA[:, j, 0, :], ps[:, j, 0:EC], ACT.Copy, scale=raw13[j][:, 2 * W13:2 * W13 + 1])
                A(zeR[0:DR, j, :], ps[0:DR, j, EC:2 * EC], ACT.Copy, scale=raw13[j][0:DR, 2 * W13 + 1:2 * W13 + 2]).then_inc(zehi_ready, 1)

            def silu(m, c, jt):
                act.wait_ge(gu_done, at(JT, m, c, jt + 1))
                if c:
                    act.wait_ge(hT_ready, at(JT, m, c, jt - 3))
                A(sg[:, jt, :], ps[:, 2 + jt, 0:EC], ACT.Silu).then_inc(sg_ready, 1)

            def weigh(m, c, j):
                act.wait_ge(down_done, at(1, m, c + 1))
                act.wait_ge(toke_ready, at(1, m, c + 1))
                act.wait_ge(flushed, at(1, m, c - 1))
                for r in range(2):
                    last = A(ye[0:EROWS, j, r, :], ps[0:EROWS, 6 + j, r * D:(r + 1) * D], ACT.Copy, scale=cwe[:, j, r:r + 1])
                last.then_inc(ye_ready, 1)

            for j in range(2):
                act.wait_ge(ld_w[j], 16)
                for c in range(2):
                    split_hi(j, c)
            for j in range(2):
                x_hi(0, j, j)
            for jt in range(JT):
                silu(0, 0, jt)
            with act.Fori(0, EXPERTS // 2 - 1) as m:
                for j in range(2):
                    for jt in range(JT):
                        silu(m, 1 + j, jt)
                        if jt == 0:
                            act.wait_ge(ld_w[j], 16 * (m + 2))
                        if jt < 2:
                            split_hi(j, jt)
                    x_hi(m, 2 + j, j)
                    weigh(m, j, j)
            for jt in range(JT):
                silu(EXPERTS // 2 - 1, 1, jt)
            for j in range(2):
                weigh(EXPERTS // 2 - 1, j, j)

        @block.gpsimd
        def _(pool):
            P = nc.gpsimd
            P.memset(mhalf[:], -0.5)
            P.memset(yA[:].bitcast(f32), 0.0)
            P.memset(yR[:].bitcast(f32), 0.0).then_inc(y_zeroed, 1)
            P.memset(qT[:], 0.0)
            P.memset(prob[:], 0.0)
            P.memset(row[:], 0.0)
            P.memset(probT[:], 0.0)
            P.memset(ones[:], 1.0)
            P.memset(seen[:], 0.0).then_inc(all_zeroed, 1)
            pool.wait_ge(all_zeroed, 1)
            n = 0

            def power(out_, tmp, in_, scale, eps):
                nonlocal n
                P.tensor_scalar(tmp, in_, scale, eps, ALU.mult, ALU.add).then_inc(pool_seq, 1)
                n += 1
                pool.wait_ge(pool_seq, n)
                return P.tensor_tensor(out_, tmp, mhalf[:], ALU.pow)

            def norm(p):
                a = slice(p % 2, p % 2 + 1)
                pool.wait_ge(mv_ready, p + 1)
                power(rstd[:, a], ve[:, a], mv[:, p % 2, 1:2], 1.0, LN_EPS).then_inc(rstd_ready, 1)

            def biased(p):
                pool.wait_ge(y_ready, p + 1)
                pool.wait_ge(bo_ready, 1)
                P.tensor_tensor(h[:, p, :], h[:, p, :], bo[:], ALU.add).then_inc(hb_ready, 1)

            def shift(p):
                pool.wait_ge(smax_ready, p + 1)
                P.tensor_tensor(sm[:, p % 2], sm[:, p % 2], smax[:, p % 2, :, None].to_broadcast([128, HEADS, TOK]), ALU.subtract).then_inc(sx_ready, 1)

            def scatter(p):
                pool.wait_ge(row_ready, p + 1)
                pool.wait_ge(cw_ready, p + 1)
                pool.wait_ge(slot_ready, p + 1)
                if p == 0:
                    pool.wait_ge(zeroed, 16 * (EXPERTS + 1))
                for k in range(TOPK):
                    P.indirect_dma_start(slots, bass.IndirectOffsetOnAxis(slot[:, p % PH, k:k + 1], 0), row[:, p % 2, k, :], None,
                                         bounds_check=EXPERTS * STRIDE - 1, oob_is_err=False).then_inc(scattered[p % 2][k], 16)

            for p in FIRST:
                norm(p)
            for s in STEPS:
                for p in embedded(s - 1) if s > -2 else ():
                    norm(p)
                if in_pairs(s + 2) and s != PH - 2:
                    shift(s + 2)
                if in_pairs(s - 1):
                    a = slice((s - 1) % 2, (s - 1) % 2 + 1)
                    pool.wait_ge(mv2_ready, s)
                    power(rstd2[:, a], ve2[:, a], mv2[:, (s - 1) % 2, 1:2], 1.0, LN_EPS).then_inc(rstd2_ready, 1)
                    pool.wait_ge(ssq_ready, s)
                    power(rrms[:, a], msq[:, a], ssq[:, a], 1.0 / D, RMS_EPS / 4).then_inc(rrms_ready, 1)
                if in_pairs(s - 2):
                    pool.wait_ge(before_done, s - 1)
                    P.tensor_tensor(seen[:], seen[:], both[:, s % 2, :], ALU.add).then_inc(seen_ready, 1)
                    scatter(s - 2)
                if in_pairs(s):
                    biased(s)
                if s == PH - 2:
                    shift(s + 2)

            for a in range(2):
                pool.wait_ge(based[a], 16 * PAIRS // 2)
            pool.wait_ge(zeroed, 16 * (EXPERTS + 1))
            with pool.Fori(0, EXPERTS // 2) as m:
                for j in range(2):
                    pool.wait_ge(ye_ready, at(1, m, j + 1))
                    pool.sem_inc(held, 1)
                    for r in range(2):
                        P.indirect_dma_start(out, bass.IndirectOffsetOnAxis(toke[:, j, r:r + 1], 0), ye[0:EROWS, j, r, :], None,
                                             bounds_check=N + STRIDE - 1, oob_is_err=True, compute_op=ALU.add).then_inc(added[j][r], 16)
                    for r in range(2):
                        pool.wait_ge(added[j][r], 16 * (m + 1))
                    pool.sem_inc(flushed, 1)

        @block.vector
        def _(dve):
            V = nc.vector
            n = 0

            def then(ins):
                nonlocal n
                n += 1
                ins.then_inc(dve_seq, 1)
                dve.wait_ge(dve_seq, n)

            def embed(p):
                dve.wait_ge(conv_done, p + 1)
                V.tensor_tensor(h[:, p, :], ps[0:PT, conv_bank(p), 0:D], posb[:], ALU.add).then_inc(h_ready, 1)
                dve.wait_ge(h_ready, p + 1)
                then(V.bn_stats(stats[:, p % 2, :], h[:, p, :]))
                V.bn_aggr(mv[:, p % 2, :], stats[:, p % 2, :]).then_inc(mv_ready, 1)

            def norm(p):
                dve.wait_ge(rstd_ready, p + 1)
                if p >= 2:
                    dve.wait_ge(yt_done, p - 1)
                V.tensor_scalar(y[:, p % 2, :], h[:, p, :], mv[:, p % 2, 0:1], rstd[:, p % 2:p % 2 + 1], ALU.subtract, ALU.mult).then_inc(y_ready, 1)

            def y_lo(p):
                dve.wait_ge(yhi_ready, p + 1)
                q, bank = p % PH, yt_bank(p)

                def two(t):
                    return t.rearrange("q (i s) -> q i s", i=2)
                V.tensor_tensor(two(yA[:, 1, q, :])[:, :, 0:TOK], two(ps[:, bank, 0:PT]), two(yA[:, 0, q, :].bitcast(f32))[:, :, 0:TOK], ALU.subtract)
                V.tensor_tensor(two(yR[DR:128, q, :])[:, :, 0:TOK], two(ps[0:DR, bank, 128:128 + PT]), two(yR[0:DR, q, :].bitcast(f32))[:, :, 0:TOK],
                                ALU.subtract).then_inc(ylo_ready, 1)

            def keys(half, some):
                for hp in some:
                    m = 2 * hp + 1
                    dve.wait_ge(qk_done, 2 * HP * half + m + 1)
                    o = ps[DH:128, (0, 1, 4, 5)[m % 4], 0:2 * PH * EVEN].rearrange("q (s t) -> q s t", t=EVEN)
                    V.tensor_scalar(kB[DH:128, hp].rearrange("q p i a t -> q (p i) a t")[:, :, 1, :], o[:, :, 0:TOK], bk[DH:128, hp:hp + 1], None,
                                    ALU.add).then_inc(k1_ready, 1)

            def soften(p):
                a = p % 2
                dve.wait_ge(s_done, p + 1)
                if p >= 2:
                    dve.wait_ge(exp_ready, p - 1)
                for b in range(2):
                    last = V.scalar_tensor_tensor(sm[:, a, 6 * b:6 * b + 6, :], ps[:, b, 0:3 * PT].rearrange("q (h t) -> q h t", t=TOK), DH ** -0.5,
                                                  mask[:, None, :].to_broadcast([128, 6, TOK]), ALU.mult, ALU.add)
                last.then_inc(sm_ready, 1)
                dve.wait_ge(sm_ready, p + 1)
                V.reduce_max(smax[:, a, :], sm[:, a], AX.X).then_inc(smax_ready, 1)

            def normalise(p):
                a = p % 2
                dve.wait_ge(exp_ready, p + 1)
                then(V.reduce_sum(ssum[:, a, :], prob[:, a, :, 0:TOK], AX.X))
                then(V.reciprocal(srec[:, a, :], ssum[:, a, :]))
                V.tensor_tensor(prob[:, a, :, 0:TOK], prob[:, a, :, 0:TOK], srec[:, a, :, None].to_broadcast([128, HEADS, TOK]), ALU.mult).then_inc(p_ready, 1)

            def residual(p):
                dve.wait_ge(wo_done, p + 1)
                dve.wait_ge(hb_ready, p + 1)
                V.tensor_tensor(h2[:, p % PH, :], ps[0:PT, 6, 0:D], h[:, p, :], ALU.add).then_inc(h2_ready, 1)
                dve.wait_ge(h2_ready, p + 1)
                then(V.bn_stats(stats2[:, p % 2, :], h2[:, p % PH, :]))
                V.bn_aggr(mv2[:, p % 2, :], stats2[:, p % 2, :]).then_inc(mv2_ready, 1)

            def norm2(p):
                dve.wait_ge(rstd2_ready, p + 1)
                V.tensor_scalar(y2[:, p % PH, :], h2[:, p % PH, :], mv2[:, p % 2, 0:1], rstd2[:, p % 2:p % 2 + 1], ALU.subtract, ALU.mult).then_inc(y2_ready, 1)

            def choose(p):
                a = p % 2
                lg = ps[0:PT, 7, 256:256 + EXPERTS]
                dve.wait_ge(lg_done, p + 1)
                then(V.max(top[:, a, :], lg))
                if p >= 2:
                    dve.wait_ge(ratio_ready, p - 1)
                V.tensor_tensor(gap[:, a:a + 1], top[:, a, 1:2], top[:, a, 0:1], ALU.subtract).then_inc(gap_ready, 1)
                then(V.max_index(topi[:, a, :], top[:, a, :], lg))
                then(V.tensor_tensor(oneh[:, a], eno[:], topi[:, a, 0:TOPK, None].to_broadcast([PT, TOPK, EXPERTS]), ALU.is_equal))
                if p >= 2:
                    dve.wait_ge(seen_ready, p - 1)
                V.tensor_tensor(both[:, a, :], oneh[:, a, 0, :], oneh[:, a, 1, :], ALU.add).then_inc(both_ready, 1)

            def place_rows(p):
                a, q = p % 2, p % PH
                dve.wait_ge(before_done, p + 1)
                V.tensor_tensor(picked[:], oneh[:, a], ps[0:PT, 7, 264:264 + EXPERTS][:, None, :].to_broadcast([PT, TOPK, EXPERTS]), ALU.mult).then_inc(before_read, 1)
                dve.wait_ge(before_read, p + 1)
                then(V.reduce_sum(place[:], picked[:], AX.X))
                V.tensor_scalar(kept[:], place[:], float(CAP), None, ALU.is_lt)
                V.tensor_scalar(far[:], place[:], float(CAP), FAR, ALU.is_ge, ALU.mult)
                then(V.scalar_tensor_tensor(slotf[:], topi[:, a, 0:TOPK], float(STRIDE), place[:], ALU.mult, ALU.add))
                then(V.tensor_tensor(slotg[:], slotf[:], far[:], ALU.add))
                V.tensor_copy(slot[:, q, :], slotg[:]).then_inc(slot_ready, 1)
                dve.wait_ge(ratio_ready, p + 1)
                then(V.tensor_scalar(wsum[:], ratio[:, a:a + 1], 1.0, None, ALU.add))
                then(V.reciprocal(share[:, 0:1], wsum[:]))
                then(V.tensor_tensor(share[:, 1:2], share[:, 0:1], ratio[:, a:a + 1], ALU.mult))
                then(V.tensor_tensor(cw[:], share[:], kept[:], ALU.mult))
                V.tensor_copy(row[:, a, :, D:D + 1], cw[:, :, None]).then_inc(cw_ready, 1)
                then(V.reduce_sum(csum[:], cw[:], AX.X))
                if p >= 2:
                    dve.wait_ge(based[a], 16 * (p // 2))
                V.scalar_tensor_tensor(base[:, a, :], y2[:, q, :], csum[:], h2[:, q, :], ALU.mult, ALU.add).then_inc(base_ready, 1)

            def split_qkv(w):
                dve.wait_ge(whi_ready, w + 1)
                V.tensor_tensor(wqkv[:, w, 1].rearrange("q c n -> q (c n)"), raw[:, 2 * QKV * w:2 * QKV * (w + 1)],
                                wqkv[:, w, 0].rearrange("q c n -> q (c n)").bitcast(f32), ALU.subtract).then_inc(wlo_ready, 1)

            V.memset(kB[:], 0.0).then_inc(kb_zeroed, 1)
            dve.wait_ge(ld_pos, 32)
            then(V.tensor_tensor(posb[:], posb[:], convb[:], ALU.add))
            embed(0)
            embed(1)
            norm(0)
            embed(2)
            norm(1)
            y_lo(0)
            embed(3)
            norm(2)
            y_lo(1)
            norm(3)
            split_qkv(0)
            y_lo(2)
            y_lo(3)
            split_qkv(1)
            dve.wait_ge(ld_const, 16 * CONST_LOADS)
            dve.wait_ge(kb_zeroed, 1)
            keys(0, range(HP // 2))
            split_qkv(2)
            keys(0, range(HP // 2, HP))
            for s in STEPS:
                if in_pairs(s + 1):
                    if s == -1:
                        soften(s + 2)
                    normalise(s + 1)
                for p in embedded(s - 1) if s > -2 else ():
                    norm(p)
                if in_pairs(s + 2) and s not in (-1, PH - 2):
                    soften(s + 2)
                if s == -1:
                    dve.wait_ge(bo_done, 1)
                    V.tensor_tensor(bo[:], ps[0:PT, 7, 0:D], bo[:], ALU.add).then_inc(bo_ready, 1)
                if s in (0, 1):
                    y_lo(PH + s)
                if in_pairs(s - 2):
                    choose(s - 2)
                if in_pairs(s - 1):
                    residual(s - 1)
                    norm2(s - 1)
                if s == PH - 2:
                    y_lo(PAIRS - 2)
                if in_pairs(s - 2):
                    place_rows(s - 2)
                if s == PH - 2:
                    y_lo(PAIRS - 1)
                for p in embedded(s):
                    embed(p)
                if s == PH - 2:
                    keys(1, range(HP))
                    soften(s + 2)

            def split_lo(m, c, j, half):
                dve.wait_ge(ehi_ready, at(2, m, c, half + 1))
                last = V.tensor_tensor(wsp[:, j, 1, half, :], raw13[j][:, half * W13:(half + 1) * W13], wsp[:, j, 0, half, :].bitcast(f32), ALU.subtract)
                if half:
                    last.then_inc(elo_ready, 1)

            def x_lo(m, c, j):
                dve.wait_ge(ld_e[j], 16 * (m + 1 + c // 2))
                dve.sem_inc(held, 1)
                V.tensor_copy(meta[:, 2 * m + c, :, :], xe[0:EROWS, j, :, D:D + 2]).then_inc(meta_ready, 1)
                dve.wait_ge(zehi_ready, at(1, m, c + 1))
                V.scalar_tensor_tensor(zeA[:, j, 1, :], ps[:, j, 0:EC], raw13[j][:, 2 * W13:2 * W13 + 1], zeA[:, j, 0, :].bitcast(f32), ALU.mult, ALU.subtract)
                V.scalar_tensor_tensor(zeR[DR:128, j, :], ps[0:DR, j, EC:2 * EC], raw13[j][0:DR, 2 * W13 + 1:2 * W13 + 2], zeR[0:DR, j, :].bitcast(f32),
                                       ALU.mult, ALU.subtract).then_inc(zelo_ready, 1)

            def gated(m, c, j, jt):
                dve.wait_ge(sg_ready, at(JT, m, c, jt + 1))
                V.tensor_tensor(hT[:, j, jt, :], sg[:, jt, :], ps[:, 2 + jt, EC:2 * EC], ALU.mult).then_inc(hT_ready, 1)

            def numbers(m, c, j):
                dve.wait_ge(ye_ready, at(1, m, c - 1))
                dve.wait_ge(flushed, at(1, m, c - 1))
                dve.sem_inc(held, 1)
                V.tensor_copy(cwe[:, j, :], meta[:, 2 * m + c, :, 0])
                V.tensor_copy(toke[:, j, :], meta[:, 2 * m + c, :, 1]).then_inc(toke_ready, 1)

            for j in range(2):
                for half in range(2):
                    split_lo(0, j, j, half)
            for j in range(2):
                x_lo(0, j, j)
            for jt in range(JT):
                gated(0, 0, 0, jt)
            with dve.Fori(0, EXPERTS // 2 - 1) as m:
                for j in range(2):
                    for jt in range(JT):
                        gated(m, 1 + j, 1 - j, jt)
                        if jt < 2:
                            split_lo(m, 2 + j, j, jt)
                    numbers(m, j, j)
                    x_lo(m, 2 + j, j)
            for jt in range(JT):
                gated(EXPERTS // 2 - 1, 1, 1, jt)
            for j in range(2):
                numbers(EXPERTS // 2 - 1, j, j)


def kernel(x, L0_tok_conv_w, L0_tok_conv_b, L0_tok_pos_table, L0_attn_W_Q, L0_attn_b_Q, L0_attn_W_K, L0_attn_b_K,
           L0_attn_W_V, L0_attn_b_V, L0_attn_W_O, L0_attn_b_O, L0_ffn_gate_w, L0_ffn_w13, L0_ffn_w2, L0_ffn_norm_w):
    import concourse.bacc as bacc
    from concourse.bass_utils import run_bass_kernel_spmd
    A = np.asarray

    px = A(x).reshape(PAIRS, 2, CHANNELS, PER_SIDE, PATCH, PER_SIDE, PATCH).transpose(0, 2, 4, 6, 1, 3, 5)
    px = px.reshape(PAIRS, KC, 128, PT).transpose(0, 2, 1, 3)
    cell = np.arange(PER_SIDE) * GRID // PER_SIDE
    ids = (cell[:, None] * GRID + cell).reshape(-1)
    pos = A(L0_tok_pos_table)[np.concatenate([ids, ids])]

    def rows(a):
        return np.broadcast_to(A(a), (PT, D))

    def parts(w):
        return np.concatenate([w[:DA], np.concatenate([w[DA:], w[DA:]])], axis=1)

    def qkv(w):
        return parts(A(w).transpose(1, 0, 2).reshape(D, QKV))

    def head_bias(b):
        return A(b).reshape(HP, 128).T

    w13 = [np.concatenate([parts(A(L0_ffn_w13)[e].T), parts(A(L0_ffn_norm_w)[e][:, None])], axis=1) for e in range(EXPERTS)]
    blank = np.zeros((STRIDE, XW), np.float32)
    blank[:, D + 1] = N + np.arange(STRIDE)
    causal = np.zeros((128, TOK), np.float32)
    tri = np.where(np.arange(TOK)[:, None] >= np.arange(TOK), 0.0, IGNORE)
    causal[0:TOK], causal[SLOT:SLOT + TOK] = tri, tri
    arrays = {
        "patches": px,
        "conv_w": A(L0_tok_conv_w).reshape(D, KC, 128).transpose(2, 1, 0),
        "conv_b": rows(L0_tok_conv_b),
        "pos": pos,
        "w_qkv": np.stack([qkv(L0_attn_W_Q), qkv(L0_attn_W_K), qkv(L0_attn_W_V)]),
        "w_o": A(L0_attn_W_O).reshape(HP, 128, D).transpose(1, 0, 2),
        "b_q": head_bias(L0_attn_b_Q), "b_k": head_bias(L0_attn_b_K), "b_v": head_bias(L0_attn_b_V),
        "b_o": rows(L0_attn_b_O),
        "gate": A(L0_ffn_gate_w).T.reshape(2, D // 2, EXPERTS).transpose(1, 0, 2),
        "w13": np.stack(w13),
        "w2": A(L0_ffn_w2).transpose(0, 2, 1).reshape(EXPERTS, JT, 128, D).transpose(0, 2, 1, 3),
        "eye": np.eye(128, dtype=np.float32),
        "causal": causal,
        "before": np.triu(np.ones((PT, PT), np.float32), 1).astype(mybir.dt.np(mybir.dt.bfloat16)),
        "expert_no": np.broadcast_to(np.arange(EXPERTS, dtype=np.float32), (PT, TOPK, EXPERTS)),
        "token_no": np.arange(N, dtype=np.float32).reshape(PAIRS, PT).T,
        "blank": blank,
    }
    nc = bacc.Bacc("TRN2", target_bir_lowering=False, num_devices=1)
    feed, args = {}, []
    for name, a in arrays.items():
        feed[name] = np.ascontiguousarray(a)
        args.append(nc.dram_tensor(name, feed[name].shape, mybir.dt.from_np(feed[name].dtype), kind="ExternalInput").ap())
    out = nc.dram_tensor("out", (N + STRIDE, D), mybir.dt.float32, kind="ExternalOutput").ap()
    vit_block(nc, *args, out)
    got = run_bass_kernel_spmd(nc, [feed], core_ids=[0])
    return got.results[0]["out"][:N].reshape(IMAGES, TOK, D)
```

```python
from contextlib import ExitStack

import numpy as np
import concourse.bass as bass
from concourse import mybir

IMAGES, CHANNELS, SIDE, PATCH = 16, 3, 112, 16
PER_SIDE = SIDE // PATCH
TOK = PER_SIDE * PER_SIDE
D = 192
DA, DR = 128, 64
HEADS, DH = 12, 64
QKV = HEADS * DH
HP = HEADS // 2
EXPERTS, TOPK, HID = 8, 2, 512
N = IMAGES * TOK
CAP = -(-5 * TOPK * N // (4 * EXPERTS))
GRID = 32

PT = 2 * TOK
PAIRS = IMAGES // 2
PH = 4
SLOT = 64
EVEN = TOK + 1
KC = CHANNELS * PATCH * PATCH // 128
STRIDE = 256
EROWS = (CAP + 1) // 2
EC = 2 * EROWS
JT = HID // 128
XW = D + 4
FAR = float(1 << 20)
LN_EPS, RMS_EPS = 1e-5, 1e-6
IGNORE = -100000.0


def vit_block(nc, patches, conv_w, conv_b, pos, w_qkv, w_o, b_q, b_k, b_v, b_o, gate, w13, w2,
              eye, causal, before, expert_no, token_no, blank, out):
    f32, f32r, bf16, u32 = mybir.dt.float32, mybir.dt.float32r, mybir.dt.bfloat16, mybir.dt.uint32
    ALU, ACT, AX = mybir.AluOpType, mybir.ActivationFunctionType, mybir.AxisListType

    slots = nc.dram_tensor("slots", [EXPERTS * STRIDE, XW], f32, kind="Internal").ap()

    with ExitStack() as ctx:
        def sb(name, shape, dt=f32):
            return ctx.enter_context(nc.sbuf_tensor(name, shape, dt))

        def sem(name):
            return ctx.enter_context(nc.semaphore(name))

        convw = sb("convw", [128, KC, D])
        posb = sb("posb", [PT, D])
        convb = sb("convb", [PT, D])
        raw = sb("raw", [128, 3 * 2 * QKV])
        wqkv = sb("wqkv", [128, 3, 2, 2, QKV], f32r)
        wos = sb("wos", [128, 2, HP, D], f32r)
        bq = sb("bq", [128, HP])
        bk = sb("bk", [128, HP])
        bv = sb("bv", [128, HP])
        bo = sb("bo", [PT, D])
        gatew = sb("gatew", [D // 2, 2, EXPERTS])
        ident = sb("ident", [128, 128])
        mask = sb("mask", [128, TOK])
        earlier = sb("earlier", [PT, PT], bf16)
        ones = sb("ones", [PT, PT], bf16)
        eno = sb("eno", [PT, TOPK, EXPERTS])
        tno = sb("tno", [PT, PAIRS])
        mhalf = sb("mhalf", [PT, 1])
        xp = sb("xp", [128, PH, KC, PT])
        h = sb("h", [PT, PAIRS, D])
        y = sb("y", [PT, 2, D])
        yA = sb("yA", [128, 2, PH, 128], f32r)
        yR = sb("yR", [128, PH, 128], f32r)
        qT = sb("qT", [128, HP, PH, 2, SLOT])
        kB = sb("kB", [128, HP, PH, 2, 2, TOK])
        v = sb("v", [128, PH, QKV])
        stats = sb("stats", [PT, 2, 6])
        mv = sb("mv", [PT, 2, 2])
        ve = sb("ve", [PT, 2])
        rstd = sb("rstd", [PT, 2])
        sm = sb("sm", [128, 2, HEADS, TOK])
        prob = sb("prob", [128, 2, HEADS, SLOT])
        smax = sb("smax", [128, 2, HEADS])
        ssum = sb("ssum", [128, 2, HEADS])
        srec = sb("srec", [128, 2, HEADS])
        probT = sb("probT", [128, HEADS, 2, TOK])
        zs = sb("zs", [128, 2, 2, HP, PT], f32r)
        bvx = sb("bvx", [128, HP, PT])
        h2 = sb("h2", [PT, PH, D])
        y2 = sb("y2", [PT, PH, D])
        y2T = sb("y2T", [D // 2, 2, PT])
        sq = sb("sq", [PT, D])
        ssq = sb("ssq", [PT, 2])
        msq = sb("msq", [PT, 2])
        rrms = sb("rrms", [PT, 2])
        stats2 = sb("stats2", [PT, 2, 6])
        mv2 = sb("mv2", [PT, 2, 2])
        ve2 = sb("ve2", [PT, 2])
        rstd2 = sb("rstd2", [PT, 2])
        row = sb("row", [PT, 2, TOPK, XW])
        top = sb("top", [PT, 2, 8])
        topi = sb("topi", [PT, 2, 8], u32)
        oneh = sb("oneh", [PT, 2, TOPK, EXPERTS])
        both = sb("both", [PT, 2, EXPERTS], bf16)
        seen = sb("seen", [PT, EXPERTS], bf16)
        gap = sb("gap", [PT, 2])
        ratio = sb("ratio", [PT, 2])
        picked = sb("picked", [PT, TOPK, EXPERTS])
        place = sb("place", [PT, TOPK])
        far = sb("far", [PT, TOPK])
        first = sb("first", [PT, 2, TOPK])
        slotf = sb("slotf", [PT, TOPK])
        slot = sb("slot", [PT, PH, TOPK], u32)
        wsum = sb("wsum", [PT, 1])
        share = sb("share", [PT, 2, TOPK])
        csum = sb("csum", [PT, 1])
        base = sb("base", [PT, 2, D])
        W13 = 2 * HID
        RAW = 2 * W13 + 2
        raw13 = [raw[:, j * RAW:(j + 1) * RAW] for j in range(2)]
        wo = raw[:, 0:HP * D].rearrange("q (c d) -> q c d", c=HP)
        wsp = wqkv[:].rearrange("q w s c n -> q (w s c n)")[:, 0:8 * W13].rearrange("q (j s c n) -> q j s c n", j=2, s=2, c=2)
        meta = sb("meta", [EROWS, EXPERTS, 2, 2])
        cwe = sb("cwe", [EROWS, 2, 2])
        toke = sb("toke", [EROWS, 2, 2], u32)
        zeA = sb("zeA", [128, 2, 2, EC], f32r)
        zeR = sb("zeR", [128, 2, EC], f32r)
        xflat = xp[:].rearrange("p a c t -> p (a c t)")
        w2s = xflat[:, 0:2 * JT * D].rearrange("p (j t d) -> p j t d", j=2, t=JT)
        xe = xflat[:, 2 * JT * D:2 * JT * D + 4 * XW].rearrange("p (j r d) -> p j r d", j=2, r=2)
        vflat = v[:].rearrange("p a n -> p (a n)")
        hT = vflat[:, 0:2 * JT * EC].rearrange("p (j t n) -> p j t n", j=2, t=JT)
        sg = vflat[:, 2 * JT * EC:2 * JT * EC + 4 * EC].rearrange("p (k n) -> p k n", k=4)
        ye = qT[:].rearrange("p a b c d -> p (a b c d)")[:, 0:4 * D].rearrange("p (j r d) -> p j r d", j=2, r=2)

        ps = ctx.enter_context(nc.psum_tensor("ps", [128, 8, 512], f32))

        ld_eye, ld_pos, ld_bias, ld_const, ld_wo, zeroed = (sem(x) for x in ("ld_eye", "ld_pos", "ld_bias", "ld_const", "ld_wo", "zeroed"))
        ld_conv = [sem(f"ld_conv{j}") for j in range(2)]
        ld_x = [sem(f"ld_x{p}") for p in range(PH)]
        ld_qkv = [sem(f"ld_qkv{w}") for w in range(3)]
        ld_w = [sem(f"ld_w{j}") for j in range(2)]
        ld_d = [sem(f"ld_d{j}") for j in range(2)]
        ld_e = [sem(f"ld_e{j}") for j in range(2)]
        y_zeroed, all_zeroed, kb_zeroed = sem("y_zeroed"), sem("all_zeroed"), sem("kb_zeroed")
        conv_done, yt_done, v_done, qk_done = (sem(x) for x in ("conv_done", "yt_done", "v_done", "qk_done"))
        s_done, pt_done, z_done, wo_done = (sem(x) for x in ("s_done", "pt_done", "z_done", "wo_done"))
        y2t_done, lg_done, before_done = (sem(x) for x in ("y2t_done", "lg_done", "before_done"))
        h_ready, mv_ready, rstd_ready, y_ready, hb_ready = (sem(x) for x in ("h_ready", "mv_ready", "rstd_ready", "y_ready", "hb_ready"))
        yhi_ready, ylo_ready, v_ready, q_ready = (sem(x) for x in ("yhi_ready", "ylo_ready", "v_ready", "q_ready"))
        k0_ready, k1_ready, whi_ready, wlo_ready = (sem(x) for x in ("k0_ready", "k1_ready", "whi_ready", "wlo_ready"))
        sm_ready, smax_ready, sx_ready, exp_ready, p_ready = (sem(x) for x in ("sm_ready", "smax_ready", "sx_ready", "exp_ready", "p_ready"))
        pt_ready, zhi_ready, z_ready, wohi_ready, wo_ready = (sem(x) for x in ("pt_ready", "zhi_ready", "z_ready", "wohi_ready", "wo_ready"))
        h2_ready, mv2_ready, rstd2_ready, y2_ready = (sem(x) for x in ("h2_ready", "mv2_ready", "rstd2_ready", "y2_ready"))
        y2T_ready, ssq_ready, rrms_ready, row_ready = (sem(x) for x in ("y2T_ready", "ssq_ready", "rrms_ready", "row_ready"))
        bvx_ready, bo_done, bo_ready = (sem(x) for x in ("bvx_ready", "bo_done", "bo_ready"))
        both_ready, gap_ready, ratio_ready = (sem(x) for x in ("both_ready", "gap_ready", "ratio_ready"))
        before_read, slot_ready, seen_ready, base_ready = (sem(x) for x in ("before_read", "slot_ready", "seen_ready", "base_ready"))
        scattered = [[sem(f"scattered{a}{k}") for k in range(TOPK)] for a in range(2)]
        based = [sem(f"based{a}") for a in range(2)]
        dve_seq, pool_seq = sem("dve_seq"), sem("pool_seq")
        et_done, gu_done, down_done = sem("et_done"), sem("gu_done"), sem("down_done")
        zehi_ready, zelo_ready, sg_ready, hT_ready = (sem(x) for x in ("zehi_ready", "zelo_ready", "sg_ready", "hT_ready"))
        ehi_ready, elo_ready, meta_ready, toke_ready, ye_ready = (sem(x) for x in ("ehi_ready", "elo_ready", "meta_ready", "toke_ready", "ye_ready"))
        added = [[sem(f"added{j}{r}") for r in range(2)] for j in range(2)]
        flushed = sem("flushed")
        held = sem("held")
        BIAS = 2
        counted = (et_done, gu_done, down_done, zehi_ready, zelo_ready, sg_ready, hT_ready, ehi_ready, elo_ready,
                   meta_ready, toke_ready, ye_ready, flushed)

        def at(per_expert, m, c, more=0):
            return 2 * per_expert * m + (BIAS + per_expert * c + more)

        BIAS_LOADS, CONST_LOADS = 3, 6
        CA = KC // 2
        FIRST, LAST = range(PH), range(PH, PAIRS)
        block = ctx.enter_context(nc.Block())

        def conv_bank(p):
            return PH + p if p < PH else 6

        def yt_bank(p):
            return p if p < PH else 7 if p < PAIRS - 2 else p % 2

        STEPS = range(-2, PAIRS + 2)

        def in_pairs(p):
            return 0 <= p < PAIRS

        def embedded(s):
            return (s + PH + 2,) if s < 2 else ()

        @block.sync
        def _(sp):
            def load_w13(e, j):
                sp.dma_start(raw13[j], w13[e]).then_inc(ld_w[j], 16)

            def load_w2(e, j):
                sp.dma_start(w2s[:, j], w2[e]).then_inc(ld_d[j], 16)

            def load_slots(e, j):
                sp.dma_start(xe[:, j], slots[bass.ds(e * STRIDE, STRIDE), :].rearrange("(p two) d -> p two d", two=2)).then_inc(ld_e[j], 16)

            sp.dma_start(convw[:, 0:CA], conv_w[:, 0:CA]).then_inc(ld_conv[0], 16)
            sp.dma_start(xp[:, 0], patches[0]).then_inc(ld_x[0], 16)
            sp.dma_start(convw[:, CA:KC], conv_w[:, CA:KC]).then_inc(ld_conv[1], 16)
            for p in FIRST[1:]:
                sp.dma_start(xp[:, p], patches[p]).then_inc(ld_x[p], 16)
            for w in range(3):
                sp.dma_start(raw[:, w * 2 * QKV:(w + 1) * 2 * QKV], w_qkv[w]).then_inc(ld_qkv[w], 16)
            for c in counted:
                sp.sem_inc(c, BIAS)
            for p in FIRST:
                sp.wait_ge(conv_done, p + 1)
                sp.dma_start(xp[:, p], patches[PH + p]).then_inc(ld_x[p], 16)
            sp.wait_ge(wlo_ready, 1)
            sp.dma_start(wo, w_o).then_inc(ld_wo, 16)
            for e in range(EXPERTS):
                sp.dma_start(slots[e * STRIDE:(e + 1) * STRIDE, :], blank).then_inc(zeroed, 16)
            sp.dma_start(out[N:N + STRIDE, :], blank[:, 0:D]).then_inc(zeroed, 16)
            sp.wait_ge(wlo_ready, 3)
            sp.wait_ge(wo_ready, 1)
            sp.wait_ge(bo_done, 1)
            for j in range(2):
                load_w13(j, j)
            sp.wait_ge(conv_done, PAIRS)
            for j in range(2):
                load_w2(j, j)
            for p in range(PAIRS):
                sp.wait_ge(base_ready, p + 1)
                sp.dma_start(out[p * PT:(p + 1) * PT, :], base[:, p % 2, :]).then_inc(based[p % 2], 16)
            for a in range(2):
                for k in range(TOPK):
                    sp.wait_ge(scattered[a][k], 16 * PAIRS // 2)
            load_slots(0, 0)
            load_slots(1, 1)

            def reload(m, c, j):
                sp.wait_ge(elo_ready, at(1, m, c + 1))
                sp.wait_ge(zelo_ready, at(1, m, c + 1))
                load_w13(2 * m + c + 2, j)
                sp.wait_ge(et_done, at(1, m, c + 1))
                sp.wait_ge(meta_ready, at(1, m, c + 1))
                load_slots(2 * m + c + 2, j)

            def reload_w2(m, c, j):
                sp.wait_ge(down_done, at(2, m, c + 1))
                load_w2(2 * m + c + 2, j)

            reload(0, 0, 0)
            reload(0, 1, 1)
            with sp.Fori(0, EXPERTS // 2 - 2) as m:
                for j in range(2):
                    reload(m, 2 + j, j)
                    reload_w2(m, j, j)
            for j in range(2):
                reload_w2(EXPERTS // 2 - 2, j, j)

        @block.tensor
        def _(pe):
            mm = nc.tensor.matmul

            def conv(p):
                pe.wait_ge(ld_x[p % PH], 16 * (1 + p // PH))
                if p >= PH:
                    pe.wait_ge(h_ready, p)
                if p == PAIRS - 1:
                    pe.wait_ge(h2_ready, 1)
                for c in range(KC):
                    if p == 0 and c == CA:
                        pe.wait_ge(ld_conv[1], 16)
                    last = mm(ps[0:PT, conv_bank(p), 0:D], xp[:, p % PH, c, :], convw[:, c, :], start=(c == 0), stop=(c == KC - 1))
                last.then_inc(conv_done, 1)

            def transpose_y(p):
                bank = yt_bank(p)
                pe.wait_ge(y_ready, p + 1)
                if p == PH:
                    pe.wait_ge(h_ready, PH)
                    pe.wait_ge(bo_ready, 1)
                elif p == PH + 1:
                    pe.wait_ge(ylo_ready, p)
                elif p > PH:
                    pe.wait_ge(sm_ready, PH)
                nc.tensor.transpose(ps[:, bank, 0:PT], y[:, p % 2, 0:DA], ident[0:PT, 0:PT])
                nc.tensor.transpose(ps[0:DR, bank, 128:128 + PT], y[:, p % 2, DA:D], ident[0:PT, 0:PT]).then_inc(yt_done, 1)

            def values(p):
                pe.wait_ge(wlo_ready, 3)
                pe.wait_ge(ylo_ready, p + 1)
                if p >= 1:
                    pe.wait_ge(pt_ready, p)
                q = p % PH
                for j in range(2):
                    c = slice(384 * j, 384 * (j + 1))
                    o = ps[:, 2 + j, 0:384]
                    mm(o, yA[:, 0, q, :], wqkv[:, 2, 0, 0, c], start=True, stop=False)
                    mm(o, yA[:, 0, q, :], wqkv[:, 2, 1, 0, c], start=False, stop=False)
                    mm(o, yA[:, 1, q, :], wqkv[:, 2, 0, 0, c], start=False, stop=False)
                    mm(o, yR[:, q, :], wqkv[:, 2, 0, 1, c], start=False, stop=False)
                    last = mm(o, yR[:, q, :], wqkv[:, 2, 1, 1, c], start=False, stop=True)
                last.then_inc(v_done, 1)

            def queries_keys(half):
                pe.wait_ge(ylo_ready, PH * (half + 1))
                for n in range(2 * HP):
                    if half and n == 2:
                        pe.wait_ge(z_ready, PH - 1)
                    w, hp = n % 2, n // 2
                    if not half and n < 2:
                        pe.wait_ge(wlo_ready, n + 1)
                    if n >= 4:
                        if w:
                            pe.wait_ge(k0_ready, HP * half + hp - 1)
                            pe.wait_ge(k1_ready, HP * half + hp - 1)
                        else:
                            pe.wait_ge(q_ready, HP * half + hp - 1)
                    c = slice(128 * hp, 128 * (hp + 1))
                    o = ps[:, (0, 1, 4, 5)[n % 4], 0:2 * PH * EVEN].rearrange("p (s t) -> p s t", t=EVEN)

                    def tokens(t):
                        return t.rearrange("p a (i s) -> p (a i) s", i=2)[:, :, 0:EVEN]
                    mm(o, wqkv[:, w, 0, 0, c], tokens(yA[:, 0]), start=True, stop=False)
                    mm(o, wqkv[:, w, 0, 0, c], tokens(yA[:, 1]), start=False, stop=False)
                    mm(o, wqkv[:, w, 1, 0, c], tokens(yA[:, 0]), start=False, stop=False)
                    mm(o, wqkv[:, w, 0, 1, c], tokens(yR[:]), start=False, stop=False)
                    mm(o, wqkv[:, w, 1, 1, c], tokens(yR[:]), start=False, stop=True).then_inc(qk_done, 1)

            def scores(p):
                if p >= 1:
                    pe.wait_ge(sm_ready, p)
                for hp in range(HP):
                    if p % PH == 0 and hp in (0, HP - 1):
                        for ready in (q_ready, k0_ready, k1_ready):
                            pe.wait_ge(ready, HP * (p // PH) + (HP - 1 if hp == 0 else HP))
                    for i in range(2):
                        last = mm(ps[SLOT * i:SLOT * (i + 1), hp // 3, (hp % 3) * PT:(hp % 3 + 1) * PT], qT[:, hp, p % PH, i, :],
                                  kB[:, hp, p % PH, i].rearrange("p a t -> p (a t)"), start=True, stop=True)
                last.then_inc(s_done, 1)

            def transpose_p(p):
                pe.wait_ge(p_ready, p + 1)
                pe.wait_ge(v_ready, p + 1)
                for hp in range(HP):
                    last = nc.tensor.transpose(ps[:, 2 + hp // 3, (hp % 3) * 128:(hp % 3 + 1) * 128],
                                               prob[:, p % 2, 2 * hp:2 * hp + 2].rearrange("p a t -> p (a t)"), ident[:])
                last.then_inc(pt_done, 1)

            def outputs(p):
                pe.wait_ge(pt_ready, p + 1)
                if p >= 1:
                    pe.wait_ge(z_ready, p)
                for hp in range(HP):
                    for a in range(2):
                        hd = 2 * hp + a
                        last = mm(ps[DH * a:DH * (a + 1), 4 + hp // 3, (hp % 3) * PT:(hp % 3 + 1) * PT],
                                  v[:, p % PH, DH * hd:DH * (hd + 1)], probT[:, hd].rearrange("p i t -> p (i t)"), start=True, stop=True)
                last.then_inc(z_done, 1)

            def project(p):
                pe.wait_ge(z_ready, p + 1)
                if p >= 1:
                    pe.wait_ge(h2_ready, p)
                pe.wait_ge(h_ready, PAIRS - 1 if p == 0 else PAIRS)
                if p == 0:
                    pe.wait_ge(wo_ready, 1)
                for c in range(HP):
                    mm(ps[0:PT, 6, 0:D], zs[:, p % 2, 0, c, :], wos[:, 0, c, :], start=(c == 0), stop=False)
                    mm(ps[0:PT, 6, 0:D], zs[:, p % 2, 0, c, :], wos[:, 1, c, :], start=False, stop=False)
                    last = mm(ps[0:PT, 6, 0:D], zs[:, p % 2, 1, c, :], wos[:, 0, c, :], start=False, stop=(c == HP - 1))
                last.then_inc(wo_done, 1)

            def transpose_y2(p):
                pe.wait_ge(y2_ready, p + 1)
                pe.wait_ge(ylo_ready, PH + 2)
                if p >= 1:
                    pe.wait_ge(before_read, p)
                for c in range(2):
                    last = nc.tensor.transpose(ps[0:D // 2, 7, c * PT:(c + 1) * PT], y2[:, p % PH, c * D // 2:(c + 1) * D // 2], ident[0:PT, 0:PT])
                last.then_inc(y2t_done, 1)

            def logits(p):
                pe.wait_ge(y2T_ready, p + 1)
                for c in range(2):
                    last = mm(ps[0:PT, 7, 256:256 + EXPERTS], y2T[:, c, :], gatew[:, c, :], start=(c == 0), stop=(c == 1))
                last.then_inc(lg_done, 1)

            def count_before(p):
                pe.wait_ge(both_ready, p + 1)
                if p >= 1:
                    pe.wait_ge(seen_ready, p)
                mm(ps[0:PT, 7, 264:264 + EXPERTS], earlier[:], both[:, p % 2, :], start=True, stop=False)
                mm(ps[0:PT, 7, 264:264 + EXPERTS], ones[:], seen[:], start=False, stop=True).then_inc(before_done, 1)

            def bias_values():
                pe.wait_ge(ld_wo, 16)
                pe.wait_ge(bvx_ready, 1)
                pe.wait_ge(h_ready, PH)
                for c in range(HP):
                    last = mm(ps[0:PT, 7, 0:D], bvx[:, c, :], wo[:, c, :], start=(c == 0), stop=(c == HP - 1))
                last.then_inc(bo_done, 1)

            pe.wait_ge(ld_conv[0], 16)
            for p in FIRST:
                conv(p)
                if p == PH - 2:
                    pe.wait_ge(ld_eye, 16)
                    transpose_y(0)
            for p in FIRST[1:]:
                transpose_y(p)
            pe.wait_ge(all_zeroed, 1)
            queries_keys(0)
            pe.wait_ge(ld_const, 16 * CONST_LOADS)
            for s in STEPS:
                if in_pairs(s):
                    transpose_p(s)
                if in_pairs(s + 2) and s != PH - 2:
                    scores(s + 2)
                if s in (0, 1, 2):
                    transpose_y(PH + s)
                if in_pairs(s - 2):
                    transpose_y2(s - 2)
                if s == PAIRS:
                    logits(s - 2)
                if in_pairs(s - 1):
                    project(s - 1)
                if in_pairs(s - 2) and s != PAIRS:
                    logits(s - 2)
                if in_pairs(s + 1):
                    values(s + 1)
                if s == -1:
                    bias_values()
                if s == PH - 2:
                    transpose_y(PAIRS - 1)
                if in_pairs(s):
                    outputs(s)
                if in_pairs(s - 2):
                    count_before(s - 2)
                for p in embedded(s):
                    conv(p)
                if s == PH - 2:
                    queries_keys(1)
                    scores(s + 2)

            def transpose_x(e, j):
                for r in range(2):
                    c = r * EROWS
                    nc.tensor.transpose(ps[:, j, c:c + EROWS], xe[0:EROWS, j, r, 0:DA], ident[0:EROWS, 0:EROWS])
                    last = nc.tensor.transpose(ps[0:DR, j, EC + c:EC + c + EROWS], xe[0:EROWS, j, r, DA:D], ident[0:EROWS, 0:EROWS])
                last.then_inc(et_done, 1)

            def gate_up(m, c, j):
                pe.wait_ge(zelo_ready, at(1, m, c + 1))
                pe.wait_ge(elo_ready, at(1, m, c + 1))
                for jt in range(JT):
                    if c:
                        pe.wait_ge(hT_ready, at(JT, m, c, jt - 3))
                    for u in range(2):
                        o = ps[:, 2 + jt, u * EC:(u + 1) * EC]
                        w = slice(u * HID + 128 * jt, u * HID + 128 * (jt + 1))
                        mm(o, wsp[:, j, 0, 0, w], zeA[:, j, 0, :], start=True, stop=False)
                        mm(o, wsp[:, j, 0, 0, w], zeA[:, j, 1, :], start=False, stop=False)
                        mm(o, wsp[:, j, 1, 0, w], zeA[:, j, 0, :], start=False, stop=False)
                        mm(o, wsp[:, j, 0, 1, w], zeR[:, j, :], start=False, stop=False)
                        last = mm(o, wsp[:, j, 1, 1, w], zeR[:, j, :], start=False, stop=True)
                    last.then_inc(gu_done, 1)

            def down(m, c, j):
                pe.wait_ge(hT_ready, at(JT, m, c + 1))
                pe.wait_ge(ld_d[j], 16 * (m + 1))
                for r in range(2):
                    pe.wait_ge(ye_ready, at(2, m, c - 1, r + 1))
                    for jt in range(JT):
                        last = mm(ps[0:EROWS, 6 + r, 0:D], hT[:, j, jt, r * EROWS:(r + 1) * EROWS], w2s[:, j, jt, :],
                                  start=(jt == 0), stop=(jt == JT - 1))
                    last.then_inc(down_done, 1)

            for j in range(2):
                pe.wait_ge(ld_e[j], 16)
                transpose_x(j, j)
            gate_up(0, 0, 0)
            with pe.Fori(0, EXPERTS // 2 - 1) as m:
                for j in range(2):
                    gate_up(m, 1 + j, 1 - j)
                    pe.wait_ge(ld_e[j], 16 * (m + 2))
                    pe.wait_ge(zelo_ready, at(1, m, 1 + j))
                    transpose_x(2 * m + 2 + j, j)
                    down(m, j, j)
            gate_up(EXPERTS // 2 - 1, 1, 1)
            for j in range(2):
                down(EXPERTS // 2 - 1, j, j)

        @block.scalar
        def _(act):
            A = nc.scalar.activation
            for dst, src in ((bv, b_v), (bq, b_q), (bk, b_k)):
                act.dma_start(dst[:], src).then_inc(ld_bias, 16)
            for dst, src in ((posb, pos), (convb, conv_b)):
                act.dma_start(dst[:], src).then_inc(ld_pos, 16)
            act.dma_start(ident[:], eye).then_inc(ld_eye, 16)
            for dst, src in ((mask, causal), (gatew, gate), (earlier, before), (bo, b_o), (eno, expert_no), (tno, token_no)):
                act.dma_start(dst[:], src).then_inc(ld_const, 16)

            def y_hi(p):
                act.wait_ge(yt_done, p + 1)
                q, bank = p % PH, yt_bank(p)
                A(yA[:, 0, q, :].rearrange("q (i s) -> q i s", i=2)[:, :, 0:TOK], ps[:, bank, 0:PT].rearrange("q (i t) -> q i t", i=2), ACT.Copy)
                A(yR[0:DR, q, :].rearrange("q (i s) -> q i s", i=2)[:, :, 0:TOK], ps[0:DR, bank, 128:128 + PT].rearrange("q (i t) -> q i t", i=2),
                  ACT.Copy).then_inc(yhi_ready, 1)

            def queries_keys(half, some):
                for n in some:
                    hp, w = n // 2, n % 2
                    act.wait_ge(qk_done, 2 * HP * half + n + 1)
                    o = ps[:, (0, 1, 4, 5)[n % 4], 0:2 * PH * EVEN].rearrange("p (s t) -> p s t", t=EVEN)
                    if w:
                        A(kB[0:DH, hp].rearrange("q p i a t -> q (p i) a t")[:, :, 0, :], o[0:DH, :, 0:TOK], ACT.Identity,
                          bias=bk[0:DH, hp:hp + 1]).then_inc(k0_ready, 1)
                    else:
                        A(qT[:, hp].rearrange("q a i s -> q (a i) s")[:, :, 0:TOK], o[:, :, 0:TOK], ACT.Identity,
                          bias=bq[:, hp:hp + 1]).then_inc(q_ready, 1)

            def split_qkv(w):
                act.wait_ge(ld_qkv[w], 16)
                A(wqkv[:, w, 0].rearrange("q c n -> q (c n)"), raw[:, 2 * QKV * w:2 * QKV * (w + 1)], ACT.Copy).then_inc(whi_ready, 1)

            def diagonal(p):
                act.wait_ge(pt_done, p + 1)
                if p >= 1:
                    act.wait_ge(z_done, p)
                for i in range(2):
                    for a in range(2):
                        last = A(probT[SLOT * i:SLOT * i + TOK, a::2, i, :].rearrange("k (b h) t -> k b h t", b=2),
                                 ps[SLOT * a:SLOT * a + TOK, 2:4, 0:384].rearrange("k b (h q) -> k b h q", q=128)[:, :, :, SLOT * i:SLOT * i + TOK],
                                 ACT.Copy)
                last.then_inc(pt_ready, 1)

            def weigh_second(p):
                act.wait_ge(gap_ready, p + 1)
                if p >= 2:
                    act.wait_ge(base_ready, p - 1)
                A(ratio[:, p % 2:p % 2 + 1], gap[:, p % 2:p % 2 + 1], ACT.Exp).then_inc(ratio_ready, 1)

            def exponentials(p):
                act.wait_ge(sx_ready, p + 1)
                if p >= 2:
                    act.wait_ge(pt_done, p - 1)
                A(prob[:, p % 2, :, 0:TOK], sm[:, p % 2], ACT.Exp).then_inc(exp_ready, 1)

            def values(p):
                act.wait_ge(v_done, p + 1)
                A(v[:, p % PH, :].rearrange("r (j n) -> r j n", j=2), ps[:, 2:4, 0:384], ACT.Copy).then_inc(v_ready, 1)

            def outputs(p):
                act.wait_ge(z_done, p + 1)
                if p >= 2:
                    act.wait_ge(wo_done, p - 1)
                A(zs[:, p % 2, 0].rearrange("q (b h) t -> q b (h t)", b=2), ps[:, 4:6, 0:3 * PT], ACT.Copy).then_inc(zhi_ready, 1)

            def squares(p):
                act.wait_ge(y2_ready, p + 1)
                if p >= 2:
                    act.wait_ge(rrms_ready, p - 1)
                A(sq[:], y2[:, p % PH, :], ACT.Square, accum_out=ssq[:, p % 2:p % 2 + 1]).then_inc(ssq_ready, 1)

            def rows(p):
                act.wait_ge(rrms_ready, p + 1)
                if p == 0:
                    act.wait_ge(ld_const, 16 * CONST_LOADS)
                if p >= 2:
                    for k in range(TOPK):
                        act.wait_ge(scattered[p % 2][k], 16 * (p // 2))
                A(row[:, p % 2, :, 0:D], y2[:, p % PH, None, :].to_broadcast([PT, TOPK, D]), ACT.Copy, scale=rrms[:, p % 2:p % 2 + 1])
                A(row[:, p % 2, :, D + 1:D + 2], tno[:, p:p + 1, None].to_broadcast([PT, TOPK, 1]), ACT.Copy).then_inc(row_ready, 1)

            def transposed_y2(p):
                act.wait_ge(y2t_done, p + 1)
                if p >= 1:
                    act.wait_ge(lg_done, p)
                A(y2T[:], ps[0:D // 2, 7, 0:2 * PT].rearrange("q (c t) -> q c t", c=2), ACT.Copy).then_inc(y2T_ready, 1)

            act.wait_ge(ld_bias, 16 * BIAS_LOADS)
            A(bvx[:], bv[:, :, None].to_broadcast([128, HP, PT]), ACT.Copy).then_inc(bvx_ready, 1)
            act.wait_ge(y_zeroed, 1)
            y_hi(0)
            y_hi(1)
            split_qkv(0)
            y_hi(2)
            y_hi(3)
            split_qkv(1)
            act.wait_ge(all_zeroed, 1)
            act.wait_ge(kb_zeroed, 1)
            queries_keys(0, range(HP))
            split_qkv(2)
            queries_keys(0, range(HP, 2 * HP))
            for s in STEPS:
                if in_pairs(s):
                    diagonal(s)
                if s in (0, 1, 2):
                    y_hi(PH + s)
                if in_pairs(s - 2):
                    transposed_y2(s - 2)
                    rows(s - 2)
                if in_pairs(s - 2):
                    weigh_second(s - 2)
                if in_pairs(s + 1):
                    values(s + 1)
                if s == -2:
                    act.wait_ge(ld_wo, 16)
                    A(wos[:, 0], wo, ACT.Copy).then_inc(wohi_ready, 1)
                if in_pairs(s + 2) and s != PH - 2:
                    exponentials(s + 2)
                if s == PH - 2:
                    y_hi(PAIRS - 1)
                if in_pairs(s):
                    outputs(s)
                if in_pairs(s - 1):
                    squares(s - 1)
                if s == PH - 2:
                    queries_keys(1, range(2 * HP))
                    exponentials(s + 2)

            def split_hi(j, c):
                A(wsp[:, j, 0, c, :], raw13[j][:, c * W13:(c + 1) * W13], ACT.Copy).then_inc(ehi_ready, 1)

            def x_hi(m, c, j):
                act.wait_ge(et_done, at(1, m, c + 1))
                A(zeA[:, j, 0, :], ps[:, j, 0:EC], ACT.Copy, scale=raw13[j][:, 2 * W13:2 * W13 + 1])
                A(zeR[0:DR, j, :], ps[0:DR, j, EC:2 * EC], ACT.Copy, scale=raw13[j][0:DR, 2 * W13 + 1:2 * W13 + 2]).then_inc(zehi_ready, 1)

            def silu(m, c, jt):
                act.wait_ge(gu_done, at(JT, m, c, jt + 1))
                if c:
                    act.wait_ge(hT_ready, at(JT, m, c, jt - 3))
                A(sg[:, jt, :], ps[:, 2 + jt, 0:EC], ACT.Silu).then_inc(sg_ready, 1)

            def weigh(m, c, j):
                act.wait_ge(toke_ready, at(1, m, c + 1))
                act.wait_ge(flushed, at(1, m, c - 1))
                for r in range(2):
                    act.wait_ge(down_done, at(2, m, c, r + 1))
                    A(ye[0:EROWS, j, r, :], ps[0:EROWS, 6 + r, 0:D], ACT.Copy, scale=cwe[:, j, r:r + 1]).then_inc(ye_ready, 1)

            for j in range(2):
                act.wait_ge(ld_w[j], 16)
                for c in range(2):
                    split_hi(j, c)
            for j in range(2):
                x_hi(0, j, j)
            for jt in range(JT):
                silu(0, 0, jt)
            with act.Fori(0, EXPERTS // 2 - 1) as m:
                for j in range(2):
                    for jt in range(JT):
                        silu(m, 1 + j, jt)
                        if jt == 0:
                            act.wait_ge(ld_w[j], 16 * (m + 2))
                        if jt < 2:
                            split_hi(j, jt)
                    x_hi(m, 2 + j, j)
                    weigh(m, j, j)
            for jt in range(JT):
                silu(EXPERTS // 2 - 1, 1, jt)
            for j in range(2):
                weigh(EXPERTS // 2 - 1, j, j)

        @block.gpsimd
        def _(pool):
            P = nc.gpsimd
            P.memset(mhalf[:], -0.5)
            P.memset(yA[:].bitcast(f32), 0.0)
            P.memset(yR[:].bitcast(f32), 0.0).then_inc(y_zeroed, 1)
            P.memset(qT[:], 0.0)
            P.memset(prob[:], 0.0)
            P.memset(row[:], 0.0)
            P.memset(probT[:], 0.0)
            P.memset(ones[:], 1.0)
            P.memset(seen[:], 0.0).then_inc(all_zeroed, 1)
            pool.wait_ge(all_zeroed, 1)
            n = 0

            def power(out_, tmp, in_, scale, eps):
                nonlocal n
                P.tensor_scalar(tmp, in_, scale, eps, ALU.mult, ALU.add).then_inc(pool_seq, 1)
                n += 1
                pool.wait_ge(pool_seq, n)
                return P.tensor_tensor(out_, tmp, mhalf[:], ALU.pow)

            def norm(p):
                a = slice(p % 2, p % 2 + 1)
                pool.wait_ge(mv_ready, p + 1)
                power(rstd[:, a], ve[:, a], mv[:, p % 2, 1:2], 1.0, LN_EPS).then_inc(rstd_ready, 1)

            def biased(p):
                pool.wait_ge(y_ready, p + 1)
                pool.wait_ge(bo_ready, 1)
                P.tensor_tensor(h[:, p, :], h[:, p, :], bo[:], ALU.add).then_inc(hb_ready, 1)

            def shift(p):
                pool.wait_ge(smax_ready, p + 1)
                P.tensor_tensor(sm[:, p % 2], sm[:, p % 2], smax[:, p % 2, :, None].to_broadcast([128, HEADS, TOK]), ALU.subtract).then_inc(sx_ready, 1)

            def scatter(p):
                pool.wait_ge(row_ready, p + 1)
                pool.wait_ge(slot_ready, p + 1)
                if p == 0:
                    pool.wait_ge(zeroed, 16 * (EXPERTS + 1))
                for k in range(TOPK):
                    P.indirect_dma_start(slots, bass.IndirectOffsetOnAxis(slot[:, p % PH, k:k + 1], 0), row[:, p % 2, k, :], None,
                                         bounds_check=EXPERTS * STRIDE - 1, oob_is_err=False).then_inc(scattered[p % 2][k], 16)

            for p in FIRST:
                norm(p)
            for s in STEPS:
                for p in embedded(s - 1) if s > -2 else ():
                    norm(p)
                if in_pairs(s + 2) and s != PH - 2:
                    shift(s + 2)
                if in_pairs(s - 1):
                    a = slice((s - 1) % 2, (s - 1) % 2 + 1)
                    pool.wait_ge(mv2_ready, s)
                    power(rstd2[:, a], ve2[:, a], mv2[:, (s - 1) % 2, 1:2], 1.0, LN_EPS).then_inc(rstd2_ready, 1)
                    pool.wait_ge(ssq_ready, s)
                    power(rrms[:, a], msq[:, a], ssq[:, a], 1.0 / D, RMS_EPS / 4).then_inc(rrms_ready, 1)
                if in_pairs(s - 2):
                    pool.wait_ge(before_done, s - 1)
                    P.tensor_tensor(seen[:], seen[:], both[:, s % 2, :], ALU.add).then_inc(seen_ready, 1)
                    scatter(s - 2)
                if in_pairs(s):
                    biased(s)
                if s == PH - 2:
                    shift(s + 2)

            for a in range(2):
                pool.wait_ge(based[a], 16 * PAIRS // 2)
            pool.wait_ge(zeroed, 16 * (EXPERTS + 1))
            with pool.Fori(0, EXPERTS // 2) as m:
                for j in range(2):
                    for r in range(2):
                        pool.wait_ge(ye_ready, at(2, m, j, r + 1))
                        pool.sem_inc(held, 1)
                        P.indirect_dma_start(out, bass.IndirectOffsetOnAxis(toke[:, j, r:r + 1], 0), ye[0:EROWS, j, r, :], None,
                                             bounds_check=N + STRIDE - 1, oob_is_err=True, compute_op=ALU.add).then_inc(added[j][r], 16)
                    for r in range(2):
                        pool.wait_ge(added[j][r], 16 * (m + 1))
                    pool.sem_inc(flushed, 1)

        @block.vector
        def _(dve):
            V = nc.vector
            n = 0

            def mark(ins):
                nonlocal n
                n += 1
                ins.then_inc(dve_seq, 1)
                return n

            def then(ins):
                dve.wait_ge(dve_seq, mark(ins))

            def embed(p):
                dve.wait_ge(conv_done, p + 1)
                V.tensor_tensor(h[:, p, :], ps[0:PT, conv_bank(p), 0:D], posb[:], ALU.add).then_inc(h_ready, 1)
                dve.wait_ge(h_ready, p + 1)
                then(V.bn_stats(stats[:, p % 2, :], h[:, p, :]))
                V.bn_aggr(mv[:, p % 2, :], stats[:, p % 2, :]).then_inc(mv_ready, 1)

            def norm(p):
                dve.wait_ge(rstd_ready, p + 1)
                if p >= 2:
                    dve.wait_ge(yt_done, p - 1)
                V.tensor_scalar(y[:, p % 2, :], h[:, p, :], mv[:, p % 2, 0:1], rstd[:, p % 2:p % 2 + 1], ALU.subtract, ALU.mult).then_inc(y_ready, 1)

            def y_lo(p):
                dve.wait_ge(yhi_ready, p + 1)
                q, bank = p % PH, yt_bank(p)

                def two(t):
                    return t.rearrange("q (i s) -> q i s", i=2)
                V.tensor_tensor(two(yA[:, 1, q, :])[:, :, 0:TOK], two(ps[:, bank, 0:PT]), two(yA[:, 0, q, :].bitcast(f32))[:, :, 0:TOK], ALU.subtract)
                V.tensor_tensor(two(yR[DR:128, q, :])[:, :, 0:TOK], two(ps[0:DR, bank, 128:128 + PT]), two(yR[0:DR, q, :].bitcast(f32))[:, :, 0:TOK],
                                ALU.subtract).then_inc(ylo_ready, 1)

            def keys(half, some):
                for hp in some:
                    m = 2 * hp + 1
                    dve.wait_ge(qk_done, 2 * HP * half + m + 1)
                    o = ps[DH:128, (0, 1, 4, 5)[m % 4], 0:2 * PH * EVEN].rearrange("q (s t) -> q s t", t=EVEN)
                    V.tensor_scalar(kB[DH:128, hp].rearrange("q p i a t -> q (p i) a t")[:, :, 1, :], o[:, :, 0:TOK], bk[DH:128, hp:hp + 1], None,
                                    ALU.add).then_inc(k1_ready, 1)

            def soften(p):
                a = p % 2
                dve.wait_ge(s_done, p + 1)
                if p >= 2:
                    dve.wait_ge(exp_ready, p - 1)
                for b in range(2):
                    last = V.scalar_tensor_tensor(sm[:, a, 6 * b:6 * b + 6, :], ps[:, b, 0:3 * PT].rearrange("q (h t) -> q h t", t=TOK), DH ** -0.5,
                                                  mask[:, None, :].to_broadcast([128, 6, TOK]), ALU.mult, ALU.add)
                last.then_inc(sm_ready, 1)
                dve.wait_ge(sm_ready, p + 1)
                V.reduce_max(smax[:, a, :], sm[:, a], AX.X).then_inc(smax_ready, 1)

            def normalise(p):
                a = p % 2
                dve.wait_ge(exp_ready, p + 1)
                then(V.reduce_sum(ssum[:, a, :], prob[:, a, :, 0:TOK], AX.X))
                then(V.reciprocal(srec[:, a, :], ssum[:, a, :]))
                V.tensor_tensor(prob[:, a, :, 0:TOK], prob[:, a, :, 0:TOK], srec[:, a, :, None].to_broadcast([128, HEADS, TOK]), ALU.mult).then_inc(p_ready, 1)

            def outputs_lo(p):
                dve.wait_ge(zhi_ready, p + 1)
                V.tensor_tensor(zs[:, p % 2, 1].rearrange("q (b h) t -> q b (h t)", b=2), ps[:, 4:6, 0:3 * PT],
                                zs[:, p % 2, 0].rearrange("q (b h) t -> q b (h t)", b=2).bitcast(f32), ALU.subtract).then_inc(z_ready, 1)

            def norm2(p):
                dve.wait_ge(rstd2_ready, p + 1)
                V.tensor_scalar(y2[:, p % PH, :], h2[:, p % PH, :], mv2[:, p % 2, 0:1], rstd2[:, p % 2:p % 2 + 1], ALU.subtract, ALU.mult).then_inc(y2_ready, 1)

            def residual_and_choose(p, r):
                a = r % 2
                lg = ps[0:PT, 7, 256:256 + EXPERTS]
                if in_pairs(p):
                    dve.wait_ge(wo_done, p + 1)
                    dve.wait_ge(hb_ready, p + 1)
                    V.tensor_tensor(h2[:, p % PH, :], ps[0:PT, 6, 0:D], h[:, p, :], ALU.add).then_inc(h2_ready, 1)
                if in_pairs(r):
                    dve.wait_ge(lg_done, r + 1)
                    largest = mark(V.max(top[:, a, :], lg))
                if in_pairs(p):
                    dve.wait_ge(h2_ready, p + 1)
                    moments = mark(V.bn_stats(stats2[:, p % 2, :], h2[:, p % PH, :]))
                if in_pairs(r):
                    dve.wait_ge(dve_seq, largest)
                    if r >= 2:
                        dve.wait_ge(ratio_ready, r - 1)
                    V.tensor_tensor(gap[:, a:a + 1], top[:, a, 1:2], top[:, a, 0:1], ALU.subtract).then_inc(gap_ready, 1)
                    indices = mark(V.max_index(topi[:, a, :], top[:, a, :], lg))
                if in_pairs(p):
                    dve.wait_ge(dve_seq, moments)
                    V.bn_aggr(mv2[:, p % 2, :], stats2[:, p % 2, :]).then_inc(mv2_ready, 1)
                if in_pairs(r):
                    dve.wait_ge(dve_seq, indices)
                    if r >= 2:
                        dve.wait_ge(seen_ready, r - 1)
                    onehot = mark(V.tensor_tensor(oneh[:, a], eno[:], topi[:, a, 0:TOPK, None].to_broadcast([PT, TOPK, EXPERTS]), ALU.is_equal))
                    V.tensor_scalar(first[:, a, :], topi[:, a, 0:TOPK], float(STRIDE), None, ALU.mult)
                    dve.wait_ge(dve_seq, onehot)
                    V.tensor_tensor(both[:, a, :], oneh[:, a, 0, :], oneh[:, a, 1, :], ALU.add).then_inc(both_ready, 1)
                    dve.wait_ge(ratio_ready, r + 1)
                    then(V.tensor_scalar(wsum[:], ratio[:, a:a + 1], 1.0, None, ALU.add))
                    then(V.reciprocal(share[:, a, 0:1], wsum[:]))
                    then(V.tensor_tensor(share[:, a, 1:2], share[:, a, 0:1], ratio[:, a:a + 1], ALU.mult))

            def place_and_normalise(r, z, p):
                a, q, b = r % 2, r % PH, p % 2
                if in_pairs(r):
                    dve.wait_ge(before_done, r + 1)
                    V.tensor_tensor(picked[:], oneh[:, a], ps[0:PT, 7, 264:264 + EXPERTS][:, None, :].to_broadcast([PT, TOPK, EXPERTS]), ALU.mult).then_inc(before_read, 1)
                if in_pairs(z):
                    outputs_lo(z)
                if in_pairs(r):
                    dve.wait_ge(before_read, r + 1)
                    placed = mark(V.reduce_sum(place[:], picked[:], AX.X))
                if in_pairs(p):
                    dve.wait_ge(exp_ready, p + 1)
                    summed = mark(V.reduce_sum(ssum[:, b, :], prob[:, b, :, 0:TOK], AX.X))
                if in_pairs(r):
                    dve.wait_ge(dve_seq, placed)
                    V.tensor_scalar(far[:], place[:], float(CAP), FAR, ALU.is_ge, ALU.mult)
                    slotted = mark(V.tensor_tensor(slotf[:], first[:, a, :], place[:], ALU.add))
                if in_pairs(p):
                    dve.wait_ge(dve_seq, summed)
                    inverse = mark(V.reciprocal(srec[:, b, :], ssum[:, b, :]))
                if in_pairs(r):
                    if r >= 2:
                        for k in range(TOPK):
                            dve.wait_ge(scattered[a][k], 16 * (r // 2))
                    weighted = mark(V.scalar_tensor_tensor(row[:, a, :, D], place[:], float(CAP), share[:, a, :], ALU.is_lt, ALU.mult))
                    dve.wait_ge(dve_seq, slotted)
                    V.tensor_tensor(slot[:, q, :], slotf[:], far[:], ALU.add).then_inc(slot_ready, 1)
                if in_pairs(p):
                    dve.wait_ge(dve_seq, inverse)
                    V.tensor_tensor(prob[:, b, :, 0:TOK], prob[:, b, :, 0:TOK], srec[:, b, :, None].to_broadcast([128, HEADS, TOK]), ALU.mult).then_inc(p_ready, 1)
                if in_pairs(r):
                    dve.wait_ge(dve_seq, weighted)
                    then(V.reduce_sum(csum[:], row[:, a, :, D], AX.X))
                    if r >= 2:
                        dve.wait_ge(based[a], 16 * (r // 2))
                    V.scalar_tensor_tensor(base[:, a, :], y2[:, q, :], csum[:], h2[:, q, :], ALU.mult, ALU.add).then_inc(base_ready, 1)

            def split_qkv(w):
                dve.wait_ge(whi_ready, w + 1)
                V.tensor_tensor(wqkv[:, w, 1].rearrange("q c n -> q (c n)"), raw[:, 2 * QKV * w:2 * QKV * (w + 1)],
                                wqkv[:, w, 0].rearrange("q c n -> q (c n)").bitcast(f32), ALU.subtract).then_inc(wlo_ready, 1)

            V.memset(kB[:], 0.0).then_inc(kb_zeroed, 1)
            dve.wait_ge(ld_pos, 32)
            then(V.tensor_tensor(posb[:], posb[:], convb[:], ALU.add))
            embed(0)
            embed(1)
            norm(0)
            embed(2)
            norm(1)
            y_lo(0)
            embed(3)
            norm(2)
            y_lo(1)
            norm(3)
            split_qkv(0)
            y_lo(2)
            y_lo(3)
            split_qkv(1)
            dve.wait_ge(ld_bias, 16 * BIAS_LOADS)
            dve.wait_ge(kb_zeroed, 1)
            keys(0, range(HP // 2))
            split_qkv(2)
            keys(0, range(HP // 2, HP))
            dve.wait_ge(ld_const, 16 * CONST_LOADS)
            for s in STEPS:
                if in_pairs(s + 2) and s != PH - 2:
                    soften(s + 2)
                if s == -2:
                    dve.wait_ge(wohi_ready, 1)
                    V.tensor_tensor(wos[:, 1], wo, wos[:, 0].bitcast(f32), ALU.subtract).then_inc(wo_ready, 1)
                for p in embedded(s - 1) if s > -2 else ():
                    norm(p)
                if s == PH - 1:
                    normalise(PH)
                if s == -1:
                    dve.wait_ge(bo_done, 1)
                    V.tensor_tensor(bo[:], ps[0:PT, 7, 0:D], bo[:], ALU.add).then_inc(bo_ready, 1)
                if s in (0, 1, 2):
                    y_lo(PH + s)
                if s == PAIRS:
                    residual_and_choose(PAIRS, s - 2)
                    residual_and_choose(s - 1, PAIRS)
                else:
                    residual_and_choose(s - 1, s - 2)
                if in_pairs(s - 1):
                    norm2(s - 1)
                if s == PH - 2:
                    y_lo(PAIRS - 1)
                place_and_normalise(s - 2, s, s + 2 if s != PH - 2 else PAIRS)
                for p in embedded(s):
                    embed(p)
                if s == PH - 2:
                    keys(1, range(HP))
                    soften(s + 2)

            def split_lo(m, c, j, half):
                dve.wait_ge(ehi_ready, at(2, m, c, half + 1))
                last = V.tensor_tensor(wsp[:, j, 1, half, :], raw13[j][:, half * W13:(half + 1) * W13], wsp[:, j, 0, half, :].bitcast(f32), ALU.subtract)
                if half:
                    last.then_inc(elo_ready, 1)

            def x_lo(m, c, j):
                dve.wait_ge(ld_e[j], 16 * (m + 1 + c // 2))
                dve.sem_inc(held, 1)
                V.tensor_copy(meta[:, 2 * m + c, :, :], xe[0:EROWS, j, :, D:D + 2]).then_inc(meta_ready, 1)
                dve.wait_ge(zehi_ready, at(1, m, c + 1))
                V.scalar_tensor_tensor(zeA[:, j, 1, :], ps[:, j, 0:EC], raw13[j][:, 2 * W13:2 * W13 + 1], zeA[:, j, 0, :].bitcast(f32), ALU.mult, ALU.subtract)
                V.scalar_tensor_tensor(zeR[DR:128, j, :], ps[0:DR, j, EC:2 * EC], raw13[j][0:DR, 2 * W13 + 1:2 * W13 + 2], zeR[0:DR, j, :].bitcast(f32),
                                       ALU.mult, ALU.subtract).then_inc(zelo_ready, 1)

            def gated(m, c, j, jt):
                dve.wait_ge(sg_ready, at(JT, m, c, jt + 1))
                V.tensor_tensor(hT[:, j, jt, :], sg[:, jt, :], ps[:, 2 + jt, EC:2 * EC], ALU.mult).then_inc(hT_ready, 1)

            def numbers(m, c, j):
                dve.wait_ge(ye_ready, at(2, m, c - 1))
                dve.wait_ge(flushed, at(1, m, c - 1))
                dve.sem_inc(held, 1)
                V.tensor_copy(cwe[:, j, :], meta[:, 2 * m + c, :, 0])
                V.tensor_copy(toke[:, j, :], meta[:, 2 * m + c, :, 1]).then_inc(toke_ready, 1)

            for j in range(2):
                for half in range(2):
                    split_lo(0, j, j, half)
            for j in range(2):
                x_lo(0, j, j)
            for jt in range(JT):
                gated(0, 0, 0, jt)
            with dve.Fori(0, EXPERTS // 2 - 1) as m:
                for j in range(2):
                    for jt in range(JT):
                        gated(m, 1 + j, 1 - j, jt)
                        if jt < 2:
                            split_lo(m, 2 + j, j, jt)
                    numbers(m, j, j)
                    x_lo(m, 2 + j, j)
            for jt in range(JT):
                gated(EXPERTS // 2 - 1, 1, 1, jt)
            for j in range(2):
                numbers(EXPERTS // 2 - 1, j, j)


def kernel(x, L0_tok_conv_w, L0_tok_conv_b, L0_tok_pos_table, L0_attn_W_Q, L0_attn_b_Q, L0_attn_W_K, L0_attn_b_K,
           L0_attn_W_V, L0_attn_b_V, L0_attn_W_O, L0_attn_b_O, L0_ffn_gate_w, L0_ffn_w13, L0_ffn_w2, L0_ffn_norm_w):
    import concourse.bacc as bacc
    from concourse.bass_utils import run_bass_kernel_spmd
    A = np.asarray

    px = A(x).reshape(PAIRS, 2, CHANNELS, PER_SIDE, PATCH, PER_SIDE, PATCH).transpose(0, 2, 4, 6, 1, 3, 5)
    px = px.reshape(PAIRS, KC, 128, PT).transpose(0, 2, 1, 3)
    cell = np.arange(PER_SIDE) * GRID // PER_SIDE
    ids = (cell[:, None] * GRID + cell).reshape(-1)
    pos = A(L0_tok_pos_table)[np.concatenate([ids, ids])]

    def rows(a):
        return np.broadcast_to(A(a), (PT, D))

    def parts(w):
        return np.concatenate([w[:DA], np.concatenate([w[DA:], w[DA:]])], axis=1)

    def qkv(w):
        return parts(A(w).transpose(1, 0, 2).reshape(D, QKV))

    def head_bias(b):
        return A(b).reshape(HP, 128).T

    w13 = [np.concatenate([parts(A(L0_ffn_w13)[e].T), parts(A(L0_ffn_norm_w)[e][:, None])], axis=1) for e in range(EXPERTS)]
    blank = np.zeros((STRIDE, XW), np.float32)
    blank[:, D + 1] = N + np.arange(STRIDE)
    causal = np.zeros((128, TOK), np.float32)
    tri = np.where(np.arange(TOK)[:, None] >= np.arange(TOK), 0.0, IGNORE)
    causal[0:TOK], causal[SLOT:SLOT + TOK] = tri, tri
    arrays = {
        "patches": px,
        "conv_w": A(L0_tok_conv_w).reshape(D, KC, 128).transpose(2, 1, 0),
        "conv_b": rows(L0_tok_conv_b),
        "pos": pos,
        "w_qkv": np.stack([qkv(L0_attn_W_Q), qkv(L0_attn_W_K), qkv(L0_attn_W_V)]),
        "w_o": A(L0_attn_W_O).reshape(HP, 128, D).transpose(1, 0, 2),
        "b_q": head_bias(L0_attn_b_Q), "b_k": head_bias(L0_attn_b_K), "b_v": head_bias(L0_attn_b_V),
        "b_o": rows(L0_attn_b_O),
        "gate": A(L0_ffn_gate_w).T.reshape(2, D // 2, EXPERTS).transpose(1, 0, 2),
        "w13": np.stack(w13),
        "w2": A(L0_ffn_w2).transpose(0, 2, 1).reshape(EXPERTS, JT, 128, D).transpose(0, 2, 1, 3),
        "eye": np.eye(128, dtype=np.float32),
        "causal": causal,
        "before": np.triu(np.ones((PT, PT), np.float32), 1).astype(mybir.dt.np(mybir.dt.bfloat16)),
        "expert_no": np.broadcast_to(np.arange(EXPERTS, dtype=np.float32), (PT, TOPK, EXPERTS)),
        "token_no": np.arange(N, dtype=np.float32).reshape(PAIRS, PT).T,
        "blank": blank,
    }
    nc = bacc.Bacc("TRN2", target_bir_lowering=False, num_devices=1)
    feed, args = {}, []
    for name, a in arrays.items():
        feed[name] = np.ascontiguousarray(a)
        args.append(nc.dram_tensor(name, feed[name].shape, mybir.dt.from_np(feed[name].dtype), kind="ExternalInput").ap())
    out = nc.dram_tensor("out", (N + STRIDE, D), mybir.dt.float32, kind="ExternalOutput").ap()
    vit_block(nc, *args, out)
    got = run_bass_kernel_spmd(nc, [feed], core_ids=[0])
    return got.results[0]["out"][:N].reshape(IMAGES, TOK, D)
```
